# Optimizing a Trainium2 kernel written in Bass

```python
import numpy as np
import jax
import jax.numpy as jnp

def _softmax(x, axis=-1):
    return jax.nn.softmax(x, axis=axis)

def _gelu(x):
    return jax.nn.gelu(x, approximate=True)

def _silu(x):
    return jax.nn.silu(x)

def _sigmoid(x):
    return jax.nn.sigmoid(x)

def _layernorm(x, axis=-1, eps=1e-05):
    m = jnp.mean(x, axis=axis, keepdims=True)
    v = jnp.var(x, axis=axis, keepdims=True)
    return (x - m) / jnp.sqrt(v + eps)

def _scatter_add(tgt, idx, src, axis=0):
    return tgt.at[idx].add(src)

def _segment_sum(src, seg, n):
    return jax.ops.segment_sum(src, seg, n)
kernel_name = 'mk_gnn_resnorm_d1_gnn_r8_f1b6d4'

def setup_inputs(seed: int=0):
    np.random.seed(seed)
    _w = jnp.asarray

    def _rec_inputs():
        import jax
        import jax.numpy as jnp
        _gk = jax.random.key(seed)
        x = -0.000202 + 1 * jax.random.normal(jax.random.fold_in(_gk, 1), (6250, 128), jnp.float32)
        src = jax.random.randint(jax.random.fold_in(_gk, 2), (200000,), 0, 6250, jnp.int32)
        dst = jax.random.randint(jax.random.fold_in(_gk, 3), (200000,), 0, 6250, jnp.int32)
        _o = jnp.argsort(dst, stable=True)
        src = src[_o]
        dst = dst[_o]
        return (x, src, dst)
    x, src, dst = _rec_inputs()

    def _L0_gnn_setup():
        import jax, jax.numpy as jnp
        import numpy as np
        N, E, D, H, L, FF = (6250, 62500, 128, 8, 2, 512)
        HD = D // H

        def _layernorm(x, g, b):
            mu = jnp.mean(x, axis=-1, keepdims=True)
            var = jnp.mean(jnp.square(x - mu), axis=-1, keepdims=True)
            return (x - mu) * jax.lax.rsqrt(var + 1e-05) * g + b

        def _forward(edge_index, x, Wq, bq, Wk, bk, Wv, bv, Wo, bo, Wpos, bpos, Wdeg, bdeg, ln1_g, ln1_b, ln2_g, ln2_b, W1, b1, W2, b2):
            n = x.shape[0]
            loops = jnp.arange(n, dtype=edge_index.dtype)
            src = jnp.concatenate([edge_index[0], loops])
            dst = jnp.concatenate([edge_index[1], loops])
            scale = np.float32(np.sqrt(HD))
            for l in range(L):
                xn = _layernorm(x, ln1_g[l], ln1_b[l])
                deg = jax.ops.segment_sum(jnp.ones_like(src, dtype=x.dtype), src, num_segments=n)
                deg = (deg - deg.mean()) / (jnp.std(deg, ddof=1) + 1e-06)
                pos = xn @ Wpos[l] + bpos[l] + deg[:, None] * Wdeg[l][0] + bdeg[l]
                xp = xn + pos
                q = (xp @ Wq[l] + bq[l]).reshape(n, H, HD)
                k = (xp @ Wk[l] + bk[l]).reshape(n, H, HD)
                v = (xp @ Wv[l] + bv[l]).reshape(n, H, HD)
                att = jnp.einsum('ehd,ehd->eh', q[dst], k[src]) / scale
                att = jnp.nan_to_num(jnp.clip(att, -50.0, 50.0), nan=0.0, posinf=50.0, neginf=-50.0)
                m = jax.ops.segment_max(att, dst, num_segments=n)
                ex = jnp.exp(att - m[dst])
                s = jax.ops.segment_sum(ex, dst, num_segments=n)
                alpha = ex / (s[dst] + 1e-16)
                msg = (v[src] * alpha[:, :, None]).reshape(-1, D)
                aggr = jax.ops.segment_sum(msg, dst, num_segments=n)
                x = x + (aggr @ Wo[l] + bo[l])
                h = jax.nn.gelu(_layernorm(x, ln2_g[l], ln2_b[l]) @ W1[l] + b1[l], approximate=False)
                x = x + (h @ W2[l] + b2[l])
            return x
        key = jax.random.key(seed)
        ks = jax.random.split(key, 16)
        inp = {'x': jax.random.normal(ks[0], (N, D), jnp.float32), 'edge_index': jax.random.randint(ks[1], (2, E), 0, N, jnp.int32)}

        def w(k, shape, fan_in):
            return jax.random.normal(k, shape, jnp.float32) / np.float32(np.sqrt(fan_in))
        inp['Wq'] = w(ks[2], (L, D, D), D)
        inp['Wk'] = w(ks[3], (L, D, D), D)
        inp['Wv'] = w(ks[4], (L, D, D), D)
        inp['Wo'] = w(ks[5], (L, D, D), D)
        inp['Wpos'] = w(ks[6], (L, D, D), D)
        inp['Wdeg'] = w(ks[7], (L, 1, D), 1)
        inp['W1'] = w(ks[8], (L, D, FF), D)
        inp['W2'] = w(ks[9], (L, FF, D), FF)
        for name, shape in [('bq', (L, D)), ('bk', (L, D)), ('bv', (L, D)), ('bo', (L, D)), ('bpos', (L, D)), ('bdeg', (L, D)), ('ln1_b', (L, D)), ('ln2_b', (L, D)), ('b1', (L, FF)), ('b2', (L, D))]:
            inp[name] = jnp.zeros(shape, jnp.float32)
        inp['ln1_g'] = jnp.ones((L, D), jnp.float32)
        inp['ln2_g'] = jnp.ones((L, D), jnp.float32)
        return inp
    _L0_gnn_all = _L0_gnn_setup()
    _L0_gnn_in = {k: v for k, v in _L0_gnn_all.items() if k in ('Wq', 'bq', 'Wk', 'bk', 'Wv', 'bv', 'Wo', 'bo', 'Wpos', 'bpos', 'Wdeg', 'bdeg', 'ln1_g', 'ln1_b', 'ln2_g', 'ln2_b', 'W1', 'b1', 'W2', 'b2')}
    del _L0_gnn_all
    return {'x': x, 'src': src, 'dst': dst, 'L0_gnn_Wq': _L0_gnn_in['Wq'], 'L0_gnn_bq': _L0_gnn_in['bq'], 'L0_gnn_Wk': _L0_gnn_in['Wk'], 'L0_gnn_bk': _L0_gnn_in['bk'], 'L0_gnn_Wv': _L0_gnn_in['Wv'], 'L0_gnn_bv': _L0_gnn_in['bv'], 'L0_gnn_Wo': _L0_gnn_in['Wo'], 'L0_gnn_bo': _L0_gnn_in['bo'], 'L0_gnn_Wpos': _L0_gnn_in['Wpos'], 'L0_gnn_bpos': _L0_gnn_in['bpos'], 'L0_gnn_Wdeg': _L0_gnn_in['Wdeg'], 'L0_gnn_bdeg': _L0_gnn_in['bdeg'], 'L0_gnn_ln1_g': _L0_gnn_in['ln1_g'], 'L0_gnn_ln1_b': _L0_gnn_in['ln1_b'], 'L0_gnn_ln2_g': _L0_gnn_in['ln2_g'], 'L0_gnn_ln2_b': _L0_gnn_in['ln2_b'], 'L0_gnn_W1': _L0_gnn_in['W1'], 'L0_gnn_b1': _L0_gnn_in['b1'], 'L0_gnn_W2': _L0_gnn_in['W2'], 'L0_gnn_b2': _L0_gnn_in['b2']}

def reference(x, src, dst, L0_gnn_Wq, L0_gnn_bq, L0_gnn_Wk, L0_gnn_bk, L0_gnn_Wv, L0_gnn_bv, L0_gnn_Wo, L0_gnn_bo, L0_gnn_Wpos, L0_gnn_bpos, L0_gnn_Wdeg, L0_gnn_bdeg, L0_gnn_ln1_g, L0_gnn_ln1_b, L0_gnn_ln2_g, L0_gnn_ln2_b, L0_gnn_W1, L0_gnn_b1, L0_gnn_W2, L0_gnn_b2):
    import jax
    import jax.numpy as jnp

    def _L0_gnn_ref(x, edge_index, Wq, bq, Wk, bk, Wv, bv, Wo, bo, Wpos, bpos, Wdeg, bdeg, ln1_g, ln1_b, ln2_g, ln2_b, W1, b1, W2, b2):
        import jax, jax.numpy as jnp
        import numpy as np
        N, E, D, H, L, FF = (6250, 62500, 128, 8, 2, 512)
        HD = D // H

        def _layernorm(x, g, b):
            mu = jnp.mean(x, axis=-1, keepdims=True)
            var = jnp.mean(jnp.square(x - mu), axis=-1, keepdims=True)
            return (x - mu) * jax.lax.rsqrt(var + 1e-05) * g + b

        def _forward(edge_index, x, Wq, bq, Wk, bk, Wv, bv, Wo, bo, Wpos, bpos, Wdeg, bdeg, ln1_g, ln1_b, ln2_g, ln2_b, W1, b1, W2, b2):
            n = x.shape[0]
            loops = jnp.arange(n, dtype=edge_index.dtype)
            src = jnp.concatenate([edge_index[0], loops])
            dst = jnp.concatenate([edge_index[1], loops])
            scale = np.float32(np.sqrt(HD))
            for l in range(L):
                xn = _layernorm(x, ln1_g[l], ln1_b[l])
                deg = jax.ops.segment_sum(jnp.ones_like(src, dtype=x.dtype), src, num_segments=n)
                deg = (deg - deg.mean()) / (jnp.std(deg, ddof=1) + 1e-06)
                pos = xn @ Wpos[l] + bpos[l] + deg[:, None] * Wdeg[l][0] + bdeg[l]
                xp = xn + pos
                q = (xp @ Wq[l] + bq[l]).reshape(n, H, HD)
                k = (xp @ Wk[l] + bk[l]).reshape(n, H, HD)
                v = (xp @ Wv[l] + bv[l]).reshape(n, H, HD)
                att = jnp.einsum('ehd,ehd->eh', q[dst], k[src]) / scale
                att = jnp.nan_to_num(jnp.clip(att, -50.0, 50.0), nan=0.0, posinf=50.0, neginf=-50.0)
                m = jax.ops.segment_max(att, dst, num_segments=n)
                ex = jnp.exp(att - m[dst])
                s = jax.ops.segment_sum(ex, dst, num_segments=n)
                alpha = ex / (s[dst] + 1e-16)
                msg = (v[src] * alpha[:, :, None]).reshape(-1, D)
                aggr = jax.ops.segment_sum(msg, dst, num_segments=n)
                x = x + (aggr @ Wo[l] + bo[l])
                h = jax.nn.gelu(_layernorm(x, ln2_g[l], ln2_b[l]) @ W1[l] + b1[l], approximate=False)
                x = x + (h @ W2[l] + b2[l])
            return x
        return _forward(edge_index, x, Wq, bq, Wk, bk, Wv, bv, Wo, bo, Wpos, bpos, Wdeg, bdeg, ln1_g, ln1_b, ln2_g, ln2_b, W1, b1, W2, b2)
    edge_index = jnp.stack([src, dst])
    x = _layernorm(x + _L0_gnn_ref(x, edge_index, L0_gnn_Wq, L0_gnn_bq, L0_gnn_Wk, L0_gnn_bk, L0_gnn_Wv, L0_gnn_bv, L0_gnn_Wo, L0_gnn_bo, L0_gnn_Wpos, L0_gnn_bpos, L0_gnn_Wdeg, L0_gnn_bdeg, L0_gnn_ln1_g, L0_gnn_ln1_b, L0_gnn_ln2_g, L0_gnn_ln2_b, L0_gnn_W1, L0_gnn_b1, L0_gnn_W2, L0_gnn_b2), axis=-1)
    return x

_drawn_inputs = setup_inputs


def setup_inputs(seed=0):
    import zlib

    import numpy as np

    out = dict(_drawn_inputs(seed))
    spreads = {'L0_gnn_bq': (0.0, 0.1),
     'L0_gnn_bk': (0.0, 0.1),
     'L0_gnn_bv': (0.0, 0.1),
     'L0_gnn_bo': (0.0, 0.1),
     'L0_gnn_bpos': (0.0, 0.1),
     'L0_gnn_bdeg': (0.0, 0.1),
     'L0_gnn_ln1_g': (1.0, 0.2),
     'L0_gnn_ln1_b': (0.0, 0.1),
     'L0_gnn_ln2_g': (1.0, 0.2),
     'L0_gnn_ln2_b': (0.0, 0.1),
     'L0_gnn_b1': (0.0, 0.1),
     'L0_gnn_b2': (0.0, 0.1)}
    factors = {}
    for name, (base, spread) in spreads.items():
        noise = np.random.default_rng([zlib.crc32(name.encode()), seed]).standard_normal(out[name].shape)
        drawn = base * np.exp(spread * noise) if base else spread * noise
        out[name] = jnp.asarray(drawn.astype(out[name].dtype))
    for name, factor in factors.items():
        out[name] = (out[name] * factor).astype(out[name].dtype)
    return out
```

```python
from contextlib import ExitStack

import concourse.bass as bass
from concourse import mybir

ALU = mybir.AluOpType
ACT = mybir.ActivationFunctionType
AX_X = mybir.AxisListType.X
F32 = mybir.dt.float32
I32 = mybir.dt.int32
BF16 = mybir.dt.bfloat16
U8 = mybir.dt.uint8

P = 128
N, D, H, L, FF, E = 6250, 128, 8, 2, 512, 200000
HD = D // H
NT = -(-N // P)
NP = NT * P
LAST = N - (NT - 1) * P
T = 8
CH = T * P
NC = -(-E // CH)
EP = NC * CH
HALF = P // 2
NW = (N - 1) // HALF + 1
QROWS = (NW - 1) * HALF + P
MW = D + H
FC = FF // P
QKV = 3 * D
FAR = 1 << 14
OUTSIDE = 255
LIMIT = 50.0
EPS = 1e-5
RING_KV = 4
WORK = 5
LAG = 2
CPT = -(-P * E // (N * CH))
HG = 32
NEWTON = 3
RSQRT_MAGIC = float(0x5F3759DF)


class Counter:

    def __init__(self, sem):
        self.sem, self.value = sem, 0


class Lane:

    def __init__(self, done):
        self.done, self.queue, self.seen = done, [], {}
        self.before, self.regular, self.general = self.queue, [], []

    def done_point(self):
        return self.done, self.done.value

    def wait(self, *points):
        for counter, value in points:
            if self.seen.get(counter, 0) < value:
                self.seen[counter] = value
                self.queue.append(lambda e, s=counter.sem, v=value: e.wait_ge(s, v))

    def do(self, instruction, *args, after=(), **kw):
        self.wait(*after)
        self.done.value += 1
        self.queue.append(lambda e: instruction(*args, **kw).then_inc(self.done.sem, 1))
        return self.done, self.done.value

    def part(self, last, instruction, *args, after=(), **kw):
        if last:
            return self.do(instruction, *args, after=after, **kw)
        self.wait(*after)
        self.queue.append(lambda e: instruction(*args, **kw))

    def dma(self, counter, start, *args, after=(), **kw):
        self.wait(*after)
        counter.value += 16
        self.queue.append(lambda e: start(*args, **kw).then_inc(counter.sem, 16))
        return counter, counter.value

    def play(self, engine, irregular):
        for step in self.before:
            step(engine)
        is_irregular = engine.value_load(irregular, min_val=0, max_val=2 * NC)
        with engine.If(is_irregular == 0):
            for step in self.regular:
                step(engine)
        with engine.Else():
            for step in self.general:
                step(engine)


class Ring:

    def __init__(self, buffers):
        self.buffers, self.free, self.turn = buffers, [()] * len(buffers), 0

    def take(self):
        i = self.turn % len(self.buffers)
        self.turn += 1
        free, self.free[i] = self.free[i], None
        assert free is not None, "the buffer is still held"
        return i, self.buffers[i], free


def graph_transformer(nc, x, src, dst, Wq, bq, Wk, bk, Wv, bv, Wo, bo, Wpos, bpos, Wdeg, bdeg,
                      ln1_g, ln1_b, ln2_g, ln2_b, W1, b1, W2, b2, out):
    with ExitStack() as ctx:
        def sb(name, shape, dt=F32):
            return ctx.enter_context(nc.sbuf_tensor(name, shape, dt))

        def counter(name):
            return Counter(ctx.enter_context(nc.semaphore(name)))

        kv_table = [nc.dram_tensor(f"kv_table{l}", [NP, 2 * D], F32).ap() for l in range(L)]
        q_table = [nc.dram_tensor(f"q_table{l}", [QROWS, D], F32).ap() for l in range(L)]
        rel_table = nc.dram_tensor("rel_table", [EP], U8).ap()
        win_table = nc.dram_tensor("win_table", [NW, 2], I32).ap()

        x_all = sb("x_all", [P, NT, D])
        acc = sb("acc", [P, NW, MW])
        kv_ring = sb("kv_ring", [P, RING_KV, T, 2 * D])
        scratch = sb("scratch", [P, 5 * CH + 2 * T * MW])
        src_idx = sb("src_idx", [P, NC * T], I32)
        rel = sb("rel", [P, NC, T])
        rel_b = sb("rel_b", [P, 2, CH], U8)
        q_win = sb("q_win", [P, 2, D])
        att = sb("att", [P, 2, T, H])
        att_ok = sb("att_ok", [P, T, H])
        att_clip = sb("att_clip", [P, T, H])
        work = sb("work", [P, WORK, 5 * P + QKV + MW + 32])
        w_qkv = sb("w_qkv", [P, L, QKV])
        b_qkv = sb("b_qkv", [P, L, QKV])
        w_pos = sb("w_pos", [P, L, D])
        w_o = sb("w_o", [P, L, D])
        w_1 = sb("w_1", [P, L, FF])
        w_2 = sb("w_2", [P, L, FC, D])
        w_deg = sb("w_deg", [NT, L, D])
        cols = sb("cols", [P, L, 8 + FC])
        rows = sb("rows", [1, L, 2, D])
        zero_rows = sb("zero_rows", [QROWS - NP, D])
        ident = sb("ident", [P, P])
        down = sb("down", [P, P])
        up = sb("up", [P, P])
        ones = sb("ones", [P, P])
        irregular = sb("irregular", [1, 1], I32)
        passes = sb("passes", [1, NC], I32)
        steps = sb("steps", [1, 1], I32)
        any_idx = sb("any_idx", [P, T], I32)
        any_dst = sb("any_dst", [P, T], I32)
        any_rel = sb("any_rel", [P, T])
        any_win = sb("any_win", [P, 2], I32)
        any_base = sb("any_base", [P, 1])
        win_rows = sb("win_rows", [1, NW, 2], I32)
        iota_i = sb("iota_i", [P, P], I32)
        iota = sb("iota", [P, P])
        part = sb("part", [P, 1])
        neg_part = sb("neg_part", [P, 1])
        window = sb("window", [1, NC], I32)
        deg_z = sb("deg_z", [P, NT])
        deg_zT = sb("deg_zT", [NT, P])
        n_bufs = 0

        def carve(size):
            nonlocal n_bufs
            n_bufs += size
            return scratch[:, n_bufs - size:n_bufs]

        onehot_ring = Ring([carve(CH).rearrange("p (t j) -> p t j", t=T) for _ in range(2)])
        onehotT_ring = Ring([carve(CH) for _ in range(2)])
        prod = carve(CH)
        msg_ring = Ring([carve(T * MW).rearrange("p (t m) -> p t m", t=T) for _ in range(2)])
        xp_all = scratch[:, 0:NT * P].rearrange("p (j n) -> p j n", j=NT)
        hist = kv_ring[:].rearrange("p a b c -> p (a b c)").bitcast(BF16)
        n_lo, n_hi = P * HG, NT * HG
        lo_ring = Ring([hist[:, i * (n_lo + n_hi):i * (n_lo + n_hi) + n_lo].rearrange("p (v g) -> p v g", g=HG)
                        for i in range(2)])
        hi_ring = Ring([hist[:, i * (n_lo + n_hi) + n_lo:(i + 1) * (n_lo + n_hi)].rearrange("p (v g) -> p v g", g=HG)
                        for i in range(2)])
        iota_rep = hist[:, 2 * (n_lo + n_hi):2 * (n_lo + n_hi) + n_lo].rearrange("p (v g) -> p v g", g=HG)
        accf = acc[:].rearrange("p w m -> p (w m)")
        hist_i = [accf[:, i * NC * T:(i + 1) * NC * T].bitcast(I32) for i in range(2)]
        hist_b = [accf[:, (4 + i) * NC * T // 2:(5 + i) * NC * T // 2].bitcast(BF16) for i in range(2)]
        dst_i = accf[:, 3 * NC * T:4 * NC * T].bitcast(I32)
        deg_w = accf[:, 5 * NC * T:5 * NC * T + 8 * NT]
        stat = accf[:, 6 * NC * T:6 * NC * T + 14 * NT]
        by_chunk = accf[0:1, 7 * NC * T:7 * NC * T + 8 * NC].rearrange("p (i c) -> p i c", i=8)
        first_i, last_i, base_i = (by_chunk[:, i, :].bitcast(I32) for i in range(3))
        base = by_chunk[:, 3, :]
        one_row = by_chunk[:, 4:8, :]
        rel_u8 = accf[:, 4 * NC * T:4 * NC * T + NC * T // 4].bitcast(U8)

        psum = ctx.enter_context(nc.psum_tensor("psum", [P, 8, 512], F32))
        q_edge_ring = Ring([psum[:, 2 * i:2 * i + 2, :].rearrange("p b n -> p (b n)") for i in range(2)])
        sum_ring = Ring([psum[:, 4, 0:MW]])
        node_ring = Ring([psum[:, 5 + i, :] for i in range(3)])
        early_ring = Ring([psum[:, i, :] for i in range(5)])

        sp, pe, act, dve, pool = (Lane(counter(n)) for n in ("sp_done", "pe_done", "act_done", "dve_done", "pool_done"))
        c_const = counter("weights_in")
        c_x = counter("x_in")
        c_src = counter("src_in")
        c_dst = counter("dst_in")
        c_rel_out = counter("rel_out")
        c_qkv_out = [counter(f"qkv_out{i}") for i in range(WORK)]
        c_zero = counter("zero_rows_out")
        c_win = counter("win_table_out")
        g_in, g_rows = counter("general_in"), counter("general_gathered")
        g_dve, g_pe, g_act = (counter(f"general_{n}") for n in ("dve", "pe", "act"))
        c_kv = [counter(f"gathered{i}") for i in range(RING_KV)]
        c_rel = [counter(f"rel_in{i}") for i in range(2)]
        c_qwin = [counter(f"q_win_in{i}") for i in range(2)]
        c_self = [counter(f"self_in{i}") for i in range(WORK)]
        c_xin = [counter(f"x_again{i}") for i in range(WORK)]
        c_out = [counter(f"out{i}") for i in range(WORK)]

        x_full = x[0:(NT - 1) * P, :].rearrange("(j p) f -> p j f", p=P)
        pad_x = dve.do(nc.vector.memset, x_all[:, NT - 1, :], 0.0)
        sp.dma(c_src, nc.sync.dma_start, src_idx[:].rearrange("p (c t) -> p c t", t=T),
                                            src.rearrange("(c p t) -> p c t", p=P, t=T))
        src_in = c_src, c_src.value
        sp.dma(c_x, nc.sync.dma_start, x_all[:, 0:NT - 1, :], x_full)
        x_in = sp.dma(c_x, nc.sync.dma_start, x_all[0:LAST, NT - 1, :], x[(NT - 1) * P:N, :], after=[pad_x])

        def const(to, what):
            sp.dma(c_const, nc.sync.dma_start, to, what, allow_slow_non_contiguous=True)

        for l in range(L):
            for i, (W, b) in enumerate(((Wq, bq), (Wk, bk), (Wv, bv))):
                const(w_qkv[:, l, i * D:(i + 1) * D], W[l])
                const(b_qkv[:, l, i * D:(i + 1) * D], b[l].partition_broadcast(P))
            const(w_pos[:, l, :], Wpos[l])
            const(w_o[:, l, :], Wo[l])
            const(w_1[:, l, :], W1[l])
            const(w_2[:, l, :, :], W2[l].rearrange("(c p) n -> p c n", p=P))
            const(w_deg[:, l, :], Wdeg[l, 0].partition_broadcast(NT))
            for i, v in enumerate((bpos, bdeg, ln1_g, ln1_b, ln2_g, ln2_b)):
                const(cols[:, l, i:i + 1], v[l].rearrange("(p a) -> p a", a=1))
            const(cols[:, l, 8:8 + FC], b1[l].rearrange("(c p) -> p c", p=P))
            const(rows[0:1, l, 0, :], bo[l:l + 1, :])
            const(rows[0:1, l, 1, :], b2[l:l + 1, :])
        weights_in = c_const, c_const.value
        chunks = dst.rearrange("(a c n) -> a c n", a=1, n=CH)
        act.dma(c_dst, nc.scalar.dma_start, first_i[0:1, :].unsqueeze(2), chunks[:, :, 0:1],
                                             allow_slow_non_contiguous=True)
        act.dma(c_dst, nc.scalar.dma_start, last_i[0:1, 0:NC - 1].unsqueeze(2), chunks[:, 0:NC - 1, CH - 1:CH],
                                             allow_slow_non_contiguous=True)
        act.dma(c_dst, nc.scalar.dma_start, last_i[0:1, NC - 1:NC], dst[E - 1:E].rearrange("(a b) -> a b", a=1))
        act.dma(c_dst, nc.scalar.dma_start, dst_i.rearrange("p (c t) -> p c t", t=T),
                                             dst.rearrange("(c p t) -> p c t", p=P, t=T))
        dst_in = c_dst, c_dst.value

        a = pool.do(nc.gpsimd.iota, iota_i[:], pattern=[[1, P]], base=0, channel_multiplier=0)
        iota_in = dve.do(nc.vector.tensor_copy, iota[:], iota_i[:], after=[a])
        rep_in = dve.do(nc.vector.tensor_copy, iota_rep, iota_i[:].unsqueeze(2).to_broadcast([P, P, HG]), after=[a])
        a = pool.do(nc.gpsimd.memset, ones[:], 1.0)
        for t_, off in ((ident, 0), (down, -HALF), (up, HALF)):
            shapes_in = pool.do(nc.gpsimd.affine_select, out=t_[:], in_=ones[:], pattern=[[1, P]], compare_op=ALU.is_equal, fill=0.0, base=-off,
                channel_multiplier=-1, after=[a])
        part_p = dve.do(nc.vector.tensor_tensor, deg_w[:, 0:P], iota[:], ident[:], ALU.mult, after=[iota_in, shapes_in])
        part_in = dve.do(nc.vector.tensor_reduce, part[:], deg_w[:, 0:P], AX_X, ALU.add, after=[part_p])
        neg_part_in = dve.do(nc.vector.tensor_scalar, neg_part[:], part[:], -1.0, None, ALU.mult, after=[part_in])
        zero_in = pool.do(nc.gpsimd.memset, zero_rows[:], 0.0)
        for l in range(L):
            zeros_out = act.dma(c_zero, nc.scalar.dma_start, q_table[l][NP:QROWS, :], zero_rows[:], after=[zero_in])
        a = pool.do(nc.gpsimd.iota, win_rows[:, :, 0], pattern=[[HALF, NW]], base=0, channel_multiplier=0)
        b = pool.do(nc.gpsimd.iota, win_rows[:, :, 1], pattern=[[1, NW]], base=0, channel_multiplier=0)
        win_out = act.dma(c_win, nc.scalar.dma_start, win_table.rearrange("(a w) b -> a w b", a=1), win_rows[:], after=[a, b])
        s1 = dve.do(nc.vector.tensor_scalar, w_qkv[:, :, 0:D], w_qkv[:, :, 0:D], HD ** -0.5, None, ALU.mult, after=[weights_in])
        s2 = dve.do(nc.vector.tensor_scalar, b_qkv[:, :, 0:D], b_qkv[:, :, 0:D], HD ** -0.5, None, ALU.mult, after=[weights_in])
        weights_in = dve.do(nc.vector.tensor_tensor, cols[:, :, 6:7], cols[:, :, 0:1], cols[:, :, 1:2], ALU.add, after=[weights_in, s1, s2])

        def rsqrt(v, y, t, after):
            a = dve.do(nc.vector.tensor_scalar, t.bitcast(I32), v.bitcast(I32), 1, None, ALU.logical_shift_right, after=after)
            a = dve.do(nc.vector.tensor_scalar, y.bitcast(I32), t.bitcast(I32), -1.0, RSQRT_MAGIC, ALU.mult, ALU.add, after=[a])
            for _ in range(NEWTON):
                if v.shape[1] == 1:
                    a = dve.do(nc.vector.tensor_scalar, t, y, y, v, ALU.mult, ALU.mult, after=[a])
                else:
                    a = dve.do(nc.vector.tensor_tensor, t, y, y, ALU.mult, after=[a])
                    a = dve.do(nc.vector.tensor_tensor, t, t, v, ALU.mult, after=[a])
                a = dve.do(nc.vector.tensor_scalar, t, t, -0.5, 1.5, ALU.mult, ALU.add, after=[a])
                a = dve.do(nc.vector.tensor_tensor, y, y, t, ALU.mult, after=[a])
            return a

        raw = stat[:, 0:6 * NT].rearrange("p (j s) -> p j s", s=6)
        mv = stat[:, 6 * NT:8 * NT].rearrange("p (j s) -> p j s", s=2)
        var0, rstd0, tmp0, shift0 = (stat[:, (8 + i) * NT:(9 + i) * NT] for i in range(4))
        for j in range(NT):
            a = dve.do(nc.vector.bn_stats, raw[:, j, :], x_all[:, j, :], after=[x_in])
        for j in range(NT):
            b = dve.do(nc.vector.bn_aggr, mv[:, j, :], raw[:, j, :], after=[a])
        a = dve.do(nc.vector.tensor_scalar, var0, mv[:, :, 1], EPS, None, ALU.add, after=[b])
        a = rsqrt(var0, rstd0, tmp0, [a])
        b = dve.do(nc.vector.tensor_tensor, shift0, mv[:, :, 0], rstd0, ALU.mult, after=[a])
        stats0 = dve.do(nc.vector.tensor_scalar, shift0, shift0, -1.0, None, ALU.mult, after=[b])

        def ws(slot):
            w = work[:, slot, :]
            f = {"row": w[:, 0:P], "col": w[:, P:2 * P], "g": w[:, 2 * P:2 * P + 4 * P], "qkv": w[:, 5 * P:5 * P + QKV]}
            o = 5 * P + QKV
            return f, w[:, o:o + MW], w[:, o + MW:o + MW + 32]

        a = dve.do(nc.vector.tensor_scalar, hist_i[0], src_idx[:], P - 1, None, ALU.bitwise_and, after=[src_in])
        b = dve.do(nc.vector.tensor_scalar, hist_i[1], src_idx[:], P.bit_length() - 1, None, ALU.logical_shift_right, after=[src_in])
        a = dve.do(nc.vector.tensor_copy, hist_b[0], hist_i[0], after=[a])
        lohi = dve.do(nc.vector.tensor_copy, hist_b[1], hist_i[1], after=[b])
        counts = psum[:, 6, 0:NT]
        n_steps = NC * T // HG

        def histogram():
            for s in range(n_steps):
                _, lo, lo_free = lo_ring.take()
                i, hi, hi_free = hi_ring.take()
                g = slice(s * HG, (s + 1) * HG)
                a = dve.do(nc.vector.tensor_tensor, lo, hist_b[0][:, g].unsqueeze(1).to_broadcast([P, P, HG]), iota_rep, ALU.is_equal,
                    after=[lohi, rep_in, *lo_free])
                a = dve.do(nc.vector.tensor_tensor, hi, hist_b[1][:, g].unsqueeze(1).to_broadcast([P, NT, HG]), iota_rep[:, 0:NT, :], ALU.is_equal,
                    after=[*hi_free])
                for k in range(HG):
                    b = pe.part(k == HG - 1, nc.tensor.matmul, counts, lo[:, :, k], hi[:, :, k],
                                start=s == 0 and k == 0, stop=s == n_steps - 1 and k == HG - 1, after=[a])
                lo_ring.free[i] = hi_ring.free[i] = [b]
                yield b

        xp_in = [None] * NT

        def norm_and_pos(l, j, ring, xhat, hT, scale, shift, after, g_col, b_col):
            a = act.do(nc.scalar.activation, xhat, x_all[:, j, :], ACT.Identity, scale=scale, bias=shift, after=after)
            yield
            i, ps, free = ring.take()
            a = pe.do(nc.tensor.transpose, ps[:, 0:P], xhat, ident[:], after=[a, shapes_in, *free])
            yield
            a = act.do(nc.scalar.activation, hT, ps[:, 0:P], ACT.Identity, scale=g_col, bias=b_col, after=[a, weights_in])
            ring.free[i] = [a]
            yield a

        work_free = [[] for _ in range(WORK)]
        work_turn = [0]

        def take_work():
            s = work_turn[0] % WORK
            work_turn[0] += 1
            return s, work_free[s]

        def early(j):
            s, free = take_work()
            f, _, _ = ws(s)
            for a in norm_and_pos(0, j, early_ring, f["row"], f["col"], rstd0[:, j:j + 1], shift0[:, j:j + 1],
                                  [stats0, *free], cols[:, 0, 2:3], cols[:, 0, 3:4]):
                yield
            i, ps, free = early_ring.take()
            pe.part(False, nc.tensor.matmul, ps[:, 0:P], w_pos[:, 0, :], f["col"], start=True, stop=False, after=[a, *free])
            a = pe.do(nc.tensor.matmul, ps[:, 0:P], ident[:], f["col"], start=False, stop=True)
            yield
            a = act.do(nc.scalar.activation, xp_all[:, j, :], ps[:, 0:P], ACT.Identity, bias=cols[:, 0, 6:7], after=[a])
            early_ring.free[i] = [a]
            work_free[s] = [a]
            xp_in[j] = a

        def pipeline(generators, width, between=None):
            waiting, active = list(generators), []
            while waiting or active:
                if waiting and len(active) < width:
                    active.append(waiting.pop(0))
                active = [g for g in active if next(g, True) is not True]
                if between is not None:
                    next(between, None)

        h_steps = histogram()
        pipeline([early(j) for j in range(NT)], WORK - 1, h_steps)
        for _ in h_steps:
            pass
        hist_done = (pe.done, pe.done.value)

        dw = [deg_w[:, i * NT:(i + 1) * NT] for i in range(8)]
        valid, deg, dev, sq, one = dw[0], dw[1], dw[2], dw[3], dw[4]
        a = pool.do(nc.gpsimd.affine_select, out=valid, in_=ones[:, 0:NT], pattern=[[-P, NT]], compare_op=ALU.is_ge,
                                              fill=0.0, base=N - 1, channel_multiplier=-1, after=[shapes_in, part_in])
        b = dve.do(nc.vector.scalar_tensor_tensor, out=deg, in0=counts, scalar=1.0, in1=valid, op0=ALU.add, op1=ALU.mult, after=[a, hist_done, part_in])
        a = dve.do(nc.vector.tensor_reduce, one[:, 0:1], deg, AX_X, ALU.add, after=[b])
        total = psum[:, 7, 0:1]
        a = pe.do(nc.tensor.matmul, total, ones[:], one[:, 0:1], start=True, stop=True, after=[a])
        a = dve.do(nc.vector.tensor_scalar, one[:, 1:2], total, -1.0 / N, None, ALU.mult, after=[a])
        a = dve.do(nc.vector.scalar_tensor_tensor, out=dev, in0=deg, scalar=one[:, 1:2], in1=valid, op0=ALU.add, op1=ALU.mult, after=[a])
        a = dve.do(nc.vector.tensor_tensor, sq, dev, dev, ALU.mult, after=[a])
        a = dve.do(nc.vector.tensor_reduce, one[:, 2:3], sq, AX_X, ALU.add, after=[a])
        a = pe.do(nc.tensor.matmul, total, ones[:], one[:, 2:3], start=True, stop=True, after=[a])
        a = dve.do(nc.vector.tensor_scalar, one[:, 3:4], total, 1.0 / (N - 1), None, ALU.mult, after=[a])
        a = rsqrt(one[:, 3:4], one[:, 4:5], one[:, 5:6], [a])
        a = dve.do(nc.vector.tensor_scalar, one[:, 6:7], one[:, 4:5], one[:, 3:4], 1e-6, ALU.mult, ALU.add, after=[a])
        a = dve.do(nc.vector.reciprocal, one[:, 7:8], one[:, 6:7], after=[a])
        a = dve.do(nc.vector.tensor_scalar, deg_z[:], dev, one[:, 7:8], None, ALU.mult, after=[a])
        a = pe.do(nc.tensor.transpose, psum[0:NT, 7, 0:P], deg_z[:], ident[:], after=[a])
        deg_in = dve.do(nc.vector.tensor_copy, deg_zT[:], psum[0:NT, 7, 0:P], after=[a])
        node_ring.free = [[deg_in]] * 3

        def qkv_tile(l, j, s, xpT, after, ring):
            f, _, _ = ws(s)
            i, ps, free = ring.take()
            a = pe.do(nc.tensor.matmul, ps[:, 0:QKV], xpT, w_qkv[:, l, :], start=True, stop=True, after=[*after, *free])
            yield
            a = dve.do(nc.vector.tensor_tensor, f["qkv"], ps[:, 0:QKV], b_qkv[:, l, :], ALU.add, after=[a])
            ring.free[i] = [a]
            rows_ = slice(j * P, (j + 1) * P)
            c = c_qkv_out[s]
            sp.dma(c, nc.sync.dma_start, q_table[l][rows_, :], f["qkv"][:, 0:D], after=[a])
            a = sp.dma(c, nc.sync.dma_start, kv_table[l][rows_, :], f["qkv"][:, D:QKV])
            work_free[s] = [a]
            tables_out[l].append(a)

        tables_out = [[], []]

        def late(j):
            s, free = take_work()
            f, _, _ = ws(s)
            a = act.do(nc.scalar.activation, f["col"][0:NT, :], w_deg[:, 0, :], ACT.Copy, scale=ident[0:NT, j:j + 1], after=[weights_in, shapes_in, *free])
            yield
            i, ps, free = early_ring.take()
            a = pe.do(nc.tensor.matmul, ps[:, 0:P], f["col"][0:NT, :], deg_zT[:], start=True, stop=True, after=[a, deg_in, *free])
            yield
            a = dve.do(nc.vector.tensor_tensor, f["row"], ps[:, 0:P], xp_all[:, j, :], ALU.add, after=[a, xp_in[j]])
            early_ring.free[i] = [a]
            yield
            yield from qkv_tile(0, j, s, f["row"], [a], early_ring)

        shift = HALF.bit_length() - 1
        a = dve.do(nc.vector.tensor_scalar, window[:], first_i, shift, None, ALU.logical_shift_right, after=[dst_in])
        a = dve.do(nc.vector.tensor_scalar, base_i, window[:], shift, None, ALU.logical_shift_left, after=[a])
        a = dve.do(nc.vector.tensor_copy, base, base_i, after=[a])
        windows_in = a
        a = dve.do(nc.vector.tensor_tensor, passes[:], last_i, base_i, ALU.subtract, after=[a])
        a = dve.do(nc.vector.tensor_scalar, passes[:], passes[:], P.bit_length() - 1, None, ALU.logical_shift_right, after=[a])
        wide = one_row[:, 0, :]
        a = dve.do(nc.vector.tensor_copy, wide, passes[:], after=[a])
        b = dve.do(nc.vector.tensor_scalar, passes[:], wide, 1.0, None, ALU.add, after=[a])
        a = dve.do(nc.vector.tensor_scalar, one_row[:, 1, :], wide, 1.0, None, ALU.add, after=[a])
        c = dve.do(nc.vector.tensor_reduce, one_row[:, 2, 0:1], one_row[:, 1, :], AX_X, ALU.add, after=[a])
        steps_in = dve.do(nc.vector.tensor_copy, steps[:], one_row[:, 2, 0:1], after=[c])
        turns = range(CPT + LAG, NC, CPT)
        late_row = one_row[:, 3, 0:len(turns)]
        d = dve.do(nc.vector.tensor_scalar, late_row, iota[0:1, 0:len(turns)], float(P), float(P), ALU.mult, ALU.add, after=[iota_in])
        d = dve.do(nc.vector.tensor_tensor, late_row, first_i[:, CPT + LAG:NC:CPT], late_row, ALU.is_lt, after=[dst_in, d])
        d = dve.do(nc.vector.tensor_reduce, one_row[:, 2, 1:2], late_row, AX_X, ALU.add, after=[d])
        d = dve.do(nc.vector.scalar_tensor_tensor, out=one_row[:, 2, 2:3], in0=one_row[:, 2, 0:1], scalar=-float(NC),
                   in1=one_row[:, 2, 1:2], op0=ALU.add, op1=ALU.add, after=[c, d])
        plan_in = dve.do(nc.vector.tensor_copy, irregular[:], one_row[:, 2, 2:3], after=[d])
        a = b
        i, ps, free = early_ring.take()
        a = pe.do(nc.tensor.matmul, ps[:, 0:NC], ones[0:1, :], base, start=True, stop=True, after=[a, shapes_in, *free])
        a = dve.do(nc.vector.tensor_tensor, rel[:], dst_i.rearrange("p (c t) -> p c t", t=T),
                                             ps[:, 0:NC].unsqueeze(2).to_broadcast([P, NC, T]), ALU.subtract, after=[a])
        early_ring.free[i] = [a]
        rel_in = a
        a = dve.do(nc.vector.tensor_scalar, rel_u8, rel[:].rearrange("p c t -> p (c t)"), float(OUTSIDE), None, ALU.min, after=[a])
        rel_out = act.dma(c_rel_out, nc.scalar.dma_start, rel_table.rearrange("(c p t) -> p c t", p=P, t=T), rel_u8.rearrange("p (c t) -> p c t", t=T),
            allow_slow_non_contiguous=True, after=[a])

        pipeline([late(j) for j in range(NT)], WORK - 1)
        acc_zero = dve.do(nc.vector.memset, accf, 0.0, after=[rel_out, hist_done, plan_in, act.done_point()])

        lanes = (sp, pe, act, dve, pool)
        for lane in lanes:
            lane.wait(plan_in, steps_in)
        early_free = [p for r in early_ring.free for p in r]
        scratch_free = [acc_zero]
        counters = [v for v in (*[lane.done for lane in lanes], *c_qkv_out, *c_kv, *c_rel, *c_qwin, *c_self, *c_xin, *c_out)]
        snapshot = ([v.value for v in counters], [dict(lane.seen) for lane in lanes], [list(w) for w in work_free],
                    [list(f) for f in node_ring.free], work_turn[0])
        kv_free, rel_free, qwin_free, att_free = [], [], [], []
        prod_free, ok_free, acc_cleared = [], [], []
        acc_in, state = {}, {}

        def begin(queues):
            values, seen, free, node_free, turn = snapshot
            for v, value in zip(counters, values):
                v.value = value
            for lane, s_, queue in zip(lanes, seen, queues):
                lane.seen, lane.queue = dict(s_), queue
            for b in range(WORK):
                work_free[b] = list(free[b])
            work_turn[0] = turn
            node_ring.free = [list(f) for f in node_free]
            for r in (q_edge_ring, sum_ring, onehot_ring, onehotT_ring, msg_ring):
                r.free, r.turn = [early_free + scratch_free] * len(r.buffers), 0
            kv_free[:] = [[hist_done]] * RING_KV
            rel_free[:], qwin_free[:], att_free[:] = [[], []], [[], []], [[], []]
            prod_free[:], ok_free[:], acc_cleared[:] = scratch_free, [], []
            acc_in["last"] = acc_zero
            del tables_out[1][:]
            state.clear()

        def load_rel(c):
            b = c % 2
            r = sp.dma(c_rel[b], nc.sync.dma_start, rel_b[:, b, :], rel_table[c * CH:(c + 1) * CH].partition_broadcast(P),
                       after=[rel_out, *rel_free[b]])
            state[c] = {"rel": r}

        def load_queries(l, c):
            b = c % 2

            def q_load():
                w = nc.sync.value_load(window[0:1, c:c + 1], min_val=0, max_val=NW - 1)
                return nc.sync.dma_start(q_win[:, b, :], q_table[l][bass.ds(w * HALF, P), :])
            state[c]["q"] = sp.dma(c_qwin[b], q_load, after=[windows_in, zeros_out, *tables_out[l], *qwin_free[b]])

        def gather(l, c):
            k = c % RING_KV
            pool.wait(src_in, *tables_out[l], *kv_free[k])
            for t in range(T):
                g = pool.dma(c_kv[k], nc.gpsimd.indirect_dma_start, kv_ring[:, k, t, :], None, kv_table[l],
                    bass.IndirectOffsetOnAxis(ap=src_idx[:, c * T + t:c * T + t + 1], axis=0))
            state.setdefault(("g", c), g)
            state[("g", c)] = g

        def onehot(c):
            i, s_, free = onehot_ring.take()
            a = dve.do(nc.vector.tensor_tensor, s_, rel[:, c, :].unsqueeze(2).to_broadcast([P, T, P]), iota[:].unsqueeze(1).to_broadcast([P, T, P]),
                ALU.is_equal, after=[rel_in, iota_in, *free])
            state[c].update(S=s_, S_i=i, S_in=a)

        def onehotT(c):
            st = state[c]
            i, sT, free = onehotT_ring.take()
            a = act.do(nc.scalar.activation, sT, rel_b[:, c % 2, :], ACT.Abs, bias=neg_part[:], after=[st["rel"], neg_part_in, *free])
            rel_free[c % 2] = [a]
            a = act.do(nc.scalar.activation, sT, sT, ACT.Relu, bias=1.0, scale=-1.0, after=[a])
            st.update(ST=sT.rearrange("p (m t) -> p m t", t=T), ST_i=i, ST_in=a)

        def spread(c):
            st = state[c]
            i, ps, free = q_edge_ring.take()
            pe.wait(st["ST_in"], st["q"], *free)
            for t in range(T):
                a = pe.part(t == T - 1, nc.tensor.matmul, ps[:, t * P:(t + 1) * P], st["ST"][:, :, t], q_win[:, c % 2, :],
                            start=True, stop=True)
            onehotT_ring.free[st["ST_i"]] = [a]
            qwin_free[c % 2] = [a]
            st.update(qe=ps, qe_i=i, qe_in=a)

        def products(c):
            st = state[c]
            k = c % RING_KV
            a = dve.do(nc.vector.tensor_tensor, prod.rearrange("p (t d) -> p t d", t=T), st["qe"].rearrange("p (t d) -> p t d", t=T),
                                                 kv_ring[:, k, :, 0:D], ALU.mult,
                       after=[st["qe_in"], state[("g", c)], *prod_free])
            q_edge_ring.free[st["qe_i"]] = [a]
            st.update(prod_in=a)

        def scores(c):
            st = state[c]
            b = c % 2
            a = dve.do(nc.vector.tensor_reduce, att[:, b, :, :].rearrange("p t h -> p (t h)"),
                                                 prod.rearrange("p (g d) -> p g d", d=HD), AX_X, ALU.add,
                       after=[st["prod_in"], *att_free[b]])
            prod_free[:] = [a]
            d = dve.do(nc.vector.tensor_tensor, att_ok[:], att[:, b], att[:, b], ALU.is_equal, after=[a, *ok_free])
            a = dve.do(nc.vector.tensor_scalar, att_clip[:], att[:, b], -LIMIT, LIMIT, ALU.max, ALU.min, after=[a, *ok_free])
            a = dve.do(nc.vector.tensor_tensor, att[:, b], att_clip[:], att_ok[:], ALU.mult, after=[a, d])
            ok_free[:] = [a]
            st.update(att_in=a)

        def weights_of(c):
            st = state[c]
            b = c % 2
            mi, m_, free = msg_ring.take()
            a = act.do(nc.scalar.activation, m_[:, :, D:MW], att[:, b], ACT.Exp, after=[st["att_in"], *free])
            att_free[b] = [a]
            st.update(m=m_, m_i=mi, ex_in=a)

        def messages(c):
            st = state[c]
            m_ = st["m"]
            k = c % RING_KV
            a = dve.do(nc.vector.tensor_tensor, m_[:, :, 0:D].rearrange("p t (h d) -> p t h d", d=HD),
                kv_ring[:, k, :, D:2 * D].rearrange("p t (h d) -> p t h d", d=HD),
                m_[:, :, D:MW].unsqueeze(3).to_broadcast([P, T, H, HD]), ALU.mult, after=[st["ex_in"]])
            kv_free[k] = [a]
            i, ps, free = sum_ring.take()
            pe.wait(a, st["S_in"], *free)
            for t in range(T):
                b = pe.part(t == T - 1, nc.tensor.matmul, ps, st["S"][:, t, :], m_[:, t, :], start=t == 0, stop=t == T - 1)
            onehot_ring.free[st["S_i"]] = [b]
            msg_ring.free[st["m_i"]] = [b]
            st.update(sum=ps, sum_i=i, sum_in=b)

        def accumulate(c):
            st = state.pop(c)

            def add():
                w = nc.vector.value_load(window[0:1, c:c + 1], min_val=0, max_val=NW - 1)
                row = acc[:, bass.ds(w, 1), :].rearrange("p a m -> p (a m)")
                return nc.vector.tensor_tensor(row, row, st["sum"], ALU.add)
            a = dve.do(add, after=[st["sum_in"], acc_in["last"], *acc_cleared])
            acc_in["last"] = a
            sum_ring.free[st["sum_i"]] = [a]

        def layer_norm_stats(j, tiny, after):
            a = dve.do(nc.vector.bn_stats, tiny[:, 0:6], x_all[:, j, :], after=after)
            a = dve.do(nc.vector.bn_aggr, tiny[:, 6:8], tiny[:, 0:6], after=[a])
            a = dve.do(nc.vector.tensor_scalar, tiny[:, 10:11], tiny[:, 7:8], EPS, None, ALU.add, after=[a])
            a = rsqrt(tiny[:, 10:11], tiny[:, 8:9], tiny[:, 11:12], [a])
            return dve.do(nc.vector.tensor_scalar, tiny[:, 9:10], tiny[:, 6:7], tiny[:, 8:9], -1.0, ALU.mult, ALU.mult, after=[a])

        def node_tile(l, j):
            s, free = take_work()
            f, own, tiny = ws(s)
            rows_ = slice(j * P, (j + 1) * P)
            sp.dma(c_self[s], nc.sync.dma_start, f["qkv"][:, 0:D], q_table[l][rows_, :], after=[*tables_out[l], *free])
            a = sp.dma(c_self[s], nc.sync.dma_start, f["qkv"][:, D:QKV], kv_table[l][rows_, :])
            yield
            yield
            sa, sok = tiny[:, 16:16 + H], tiny[:, 24:24 + H]
            a = dve.do(nc.vector.tensor_tensor, f["row"], f["qkv"][:, 0:D], f["qkv"][:, D:2 * D], ALU.mult, after=[a])
            a = dve.do(nc.vector.tensor_reduce, sa, f["row"].rearrange("p (h d) -> p h d", d=HD), AX_X, ALU.add, after=[a])
            b = dve.do(nc.vector.tensor_tensor, sok, sa, sa, ALU.is_equal, after=[a])
            a = dve.do(nc.vector.tensor_scalar, sa, sa, -LIMIT, LIMIT, ALU.max, ALU.min, after=[a, b])
            a = dve.do(nc.vector.tensor_tensor, sa, sa, sok, ALU.mult, after=[a, b])
            a = act.do(nc.scalar.activation, own[:, D:MW], sa, ACT.Exp, after=[a])
            yield
            a = dve.do(nc.vector.tensor_tensor, own[:, 0:D].rearrange("p (h d) -> p h d", d=HD),
                                                 f["qkv"][:, 2 * D:QKV].rearrange("p (h d) -> p h d", d=HD),
                                                 own[:, D:MW].unsqueeze(2).to_broadcast([P, H, HD]), ALU.mult, after=[a])
            yield
            i, ps, free = node_ring.take()
            parts = [(ident, acc[:, 2 * j, :])]
            if j > 0:
                parts.append((down, acc[:, 2 * j - 1, :]))
            if 2 * j + 1 < NW:
                parts.append((up, acc[:, 2 * j + 1, :]))
            pe.wait(a, acc_in["last"], *free)
            pe.part(False, nc.tensor.matmul, ps[:, 0:MW], ident[:], own, start=True, stop=False)
            for n, (m_, what) in enumerate(parts):
                a = pe.part(n == len(parts) - 1, nc.tensor.matmul, ps[:, 0:MW], m_[:], what, start=False,
                            stop=n == len(parts) - 1)
            yield
            if l + 1 < L:
                done = slice(max(2 * j - 1, 0), 2 * j + 1 if j < NT - 1 else NW)
                b = act.do(nc.scalar.memzero, acc[:, done, :], after=[a])
                acc_cleared[:] = [b]
            den = tiny[:, 0:H]
            b = dve.do(nc.vector.tensor_scalar, den, ps[:, D:MW], 1e-16, None, ALU.mult, after=[a])
            b = dve.do(nc.vector.tensor_tensor, den, den, ps[:, D:MW], ALU.add, after=[b])
            b = dve.do(nc.vector.reciprocal, den, den, after=[b])
            a = dve.do(nc.vector.tensor_tensor, f["row"].rearrange("p (h d) -> p h d", d=HD),
                                                 ps[:, 0:D].rearrange("p (h d) -> p h d", d=HD),
                                                 den.unsqueeze(2).to_broadcast([P, H, HD]), ALU.mult, after=[b])
            node_ring.free[i] = [a]
            yield
            i, ps, free = node_ring.take()
            a = pe.do(nc.tensor.transpose, ps[:, 0:P], f["row"], ident[:], after=[a, *free])
            yield
            a = act.do(nc.scalar.copy, f["col"], ps[:, 0:P], after=[a])
            node_ring.free[i] = [a]
            yield
            i, ps, free = node_ring.take()
            pe.part(False, nc.tensor.matmul, ps[:, 0:D], ones[0:1, :], rows[0:1, l, 0, :], start=True, stop=False, after=[a, *free])
            a = pe.do(nc.tensor.matmul, ps[:, 0:D], f["col"], w_o[:, l, :], start=False, stop=True)
            yield
            a = dve.do(nc.vector.tensor_tensor, x_all[:, j, :], x_all[:, j, :], ps[:, 0:D], ALU.add, after=[a])
            node_ring.free[i] = [a]
            b = layer_norm_stats(j, tiny, [a])
            for a in norm_and_pos(l, j, node_ring, f["row"], f["col"], tiny[:, 8:9], tiny[:, 9:10], [b],
                                  cols[:, l, 4:5], cols[:, l, 5:6]):
                yield
            i, ps, free = node_ring.take()
            pe.wait(a, *free)
            for n in range(FC):
                a = pe.part(n == FC - 1, nc.tensor.matmul, ps[:, n * P:(n + 1) * P], w_1[:, l, n * P:(n + 1) * P], f["col"],
                            start=True, stop=True)
            yield
            for n in range(FC):
                g = act.do(nc.scalar.activation, f["g"][:, n * P:(n + 1) * P], ps[:, n * P:(n + 1) * P], ACT.Gelu,
                                                       bias=cols[:, l, 8 + n:9 + n], after=[a])
            node_ring.free[i] = [g]
            yield
            i, ps, free = node_ring.take()
            pe.part(False, nc.tensor.matmul, ps[:, 0:D], ones[0:1, :], rows[0:1, l, 1, :], start=True, stop=False, after=[g, *free])
            for n in range(FC):
                a = pe.part(n == FC - 1, nc.tensor.matmul, ps[:, 0:D], f["g"][:, n * P:(n + 1) * P], w_2[:, l, n, :],
                            start=False, stop=n == FC - 1)
            yield
            a = dve.do(nc.vector.tensor_tensor, x_all[:, j, :], x_all[:, j, :], ps[:, 0:D], ALU.add, after=[a])
            node_ring.free[i] = [a]
            if l + 1 < L:
                b = layer_norm_stats(j, tiny, [a])
                for a in norm_and_pos(l + 1, j, node_ring, f["row"], f["col"], tiny[:, 8:9], tiny[:, 9:10], [b],
                                      cols[:, l + 1, 2:3], cols[:, l + 1, 3:4]):
                    yield
                b = act.do(nc.scalar.activation, f["g"][0:NT, 0:D], w_deg[:, l + 1, :], ACT.Copy, scale=ident[0:NT, j:j + 1], after=[a])
                yield
                i, ps, free = node_ring.take()
                pe.part(False, nc.tensor.matmul, ps[:, 0:P], w_pos[:, l + 1, :], f["col"], start=True, stop=False, after=[a, *free])
                pe.part(False, nc.tensor.matmul, ps[:, 0:P], ident[:], f["col"], start=False, stop=False)
                a = pe.do(nc.tensor.matmul, ps[:, 0:P], f["g"][0:NT, 0:D], deg_zT[:], start=False, stop=True, after=[b])
                yield
                a = act.do(nc.scalar.activation, f["row"], ps[:, 0:P], ACT.Identity, bias=cols[:, l + 1, 6:7], after=[a])
                node_ring.free[i] = [a]
                yield
                yield from qkv_tile(l + 1, j, s, f["row"], [a], node_ring)
            else:
                n = P if j < NT - 1 else LAST
                b = sp.dma(c_xin[s], nc.sync.dma_start, f["row"][0:n, :], x[j * P:j * P + n, :], after=[a])
                yield
                yield
                a = dve.do(nc.vector.tensor_tensor, x_all[0:n, j, :], x_all[0:n, j, :], f["row"][0:n, :], ALU.add, after=[a, b])
                b = layer_norm_stats(j, tiny, [a])
                a = dve.do(nc.vector.tensor_scalar, f["col"], x_all[:, j, :], tiny[:, 8:9], tiny[:, 9:10], ALU.mult, ALU.add, after=[b])
                a = sp.dma(c_out[s], nc.sync.dma_start, out[j * P:j * P + n, :], f["col"][0:n, :], after=[a])
                work_free[s] = [a]

        def outputs_written():
            sp.wait(*[(c, c.value) for c in (*c_out, *c_qkv_out)], rel_out, zeros_out, win_out)

        DVE_OPS = 11

        def general_edges(l):
            any_S, any_ST, any_dst_b = onehot_ring.buffers[0], onehotT_ring.buffers[0], onehot_ring.buffers[1]
            any_dst_b = any_dst_b.rearrange("p t j -> p (t j)").bitcast(I32)
            any_msg, any_q, any_sum = msg_ring.buffers[0], q_edge_ring.buffers[0], sum_ring.buffers[0]
            rows_in = kv_ring[:, 0, :, :]
            q0, score = q_win[:, 0, :], att[:, 0]
            N_IN = 5

            def load_steps(e):
                n = general_n[e]
                window_number = e.alloc_register(f"window_number{l}")
                with e.Fori(0, NC) as c:
                    chunk = e.snap(c)
                    w0 = e.value_load(window[0:1, bass.ds(chunk, 1)], min_val=0, max_val=NW - 1)
                    count = e.value_load(passes[0:1, bass.ds(chunk, 1)], min_val=1, max_val=NT)
                    e.reg_mov(window_number, w0)
                    with e.Fori(0, count):
                        e.wait_ge(g_dve.sem, e.snap(n) * DVE_OPS + 1)
                        w = e.snap(window_number, min_val=0, max_val=NW - 1)
                        edges = bass.ds(chunk * CH, CH)
                        for to, what in ((any_idx[:], src[edges].rearrange("(p t) -> p t", p=P)),
                                         (any_dst[:], dst[edges].rearrange("(p t) -> p t", p=P)),
                                         (any_dst_b, dst[edges].partition_broadcast(P)),
                                         (any_win[:], win_table[bass.ds(w, 1), :].rearrange("a b -> (a b)").partition_broadcast(P)),
                                         (q0, q_table[l][bass.ds(w * HALF, P), :])):
                            e.dma_start(to, what).then_inc(g_in.sem, 16)
                        e.reg_add(window_number, window_number, 2)
                        e.reg_add(n, n, 1)

            def over_steps(e, body):
                n = general_n[e]
                total = e.value_load(steps[0:1, 0:1], min_val=NC, max_val=NC + NW)
                with e.Fori(0, total):
                    body(e, e.snap(n))

            def gather_step(e, n):
                e.wait_ge(g_in.sem, n * (16 * N_IN) + 16 * N_IN)
                e.reg_add(general_n[e], general_n[e], 1)
                for t in range(T):
                    e.indirect_dma_start(rows_in[:, t, :], None, kv_table[l],
                                         bass.IndirectOffsetOnAxis(ap=any_idx[:, t:t + 1], axis=0)).then_inc(g_rows.sem, 16)

            def product_step(e, n):
                e.wait_ge(g_dve.sem, n * DVE_OPS + 5)
                e.wait_ge(g_in.sem, n * (16 * N_IN) + 16 * N_IN)
                ST = any_ST.rearrange("p (m t) -> p m t", t=T)
                for t in range(T):
                    last = e.matmul(any_q[:, t * P:(t + 1) * P], ST[:, :, t], q0, start=True, stop=True)
                last.then_inc(g_pe.sem, 1)
                e.wait_ge(g_dve.sem, n * DVE_OPS + 11)
                for t in range(T):
                    last = e.matmul(any_sum, any_S[:, t, :], any_msg[:, t, :], start=t == 0, stop=t == T - 1)
                last.then_inc(g_pe.sem, 1)
                e.reg_add(general_n[e], general_n[e], 1)

            def exp_step(e, n):
                e.wait_ge(g_dve.sem, n * DVE_OPS + 10)
                e.activation(any_msg[:, :, D:MW], score, ACT.Exp).then_inc(g_act.sem, 1)
                e.reg_add(general_n[e], general_n[e], 1)

            def vector_step(e, n):
                done = [1]

                def op(instruction, *args):
                    instruction(*args).then_inc(g_dve.sem, 1)
                    done[0] += 1
                    e.wait_ge(g_dve.sem, n * DVE_OPS + done[0])

                e.wait_ge(g_in.sem, n * (16 * N_IN) + 16 * N_IN)
                op(e.tensor_copy, any_base[:], any_win[:, 0:1])
                op(e.tensor_scalar, any_rel[:], any_dst[:], any_base[:], None, ALU.subtract)
                op(e.tensor_tensor, any_S, any_rel[:].unsqueeze(2).to_broadcast([P, T, P]),
                   iota[:].unsqueeze(1).to_broadcast([P, T, P]), ALU.is_equal)
                op(e.tensor_scalar, any_ST, any_dst_b, any_base[:], part[:], ALU.subtract, ALU.is_equal)
                e.wait_ge(g_pe.sem, n * 2 + 1)
                e.wait_ge(g_rows.sem, n * (16 * T) + 16 * T)
                op(e.tensor_tensor, prod.rearrange("p (t d) -> p t d", t=T), any_q.rearrange("p (t d) -> p t d", t=T),
                   rows_in[:, :, 0:D], ALU.mult)
                op(e.tensor_reduce, score.rearrange("p t h -> p (t h)"), prod.rearrange("p (g d) -> p g d", d=HD), AX_X, ALU.add)
                op(e.tensor_tensor, att_ok[:], score, score, ALU.is_equal)
                op(e.tensor_scalar, score, score, -LIMIT, LIMIT, ALU.max, ALU.min)
                op(e.tensor_tensor, score, score, att_ok[:], ALU.mult)
                e.wait_ge(g_act.sem, n + 1)
                op(e.tensor_tensor, any_msg[:, :, 0:D].rearrange("p t (h d) -> p t h d", d=HD),
                   rows_in[:, :, D:2 * D].rearrange("p t (h d) -> p t h d", d=HD),
                   any_msg[:, :, D:MW].unsqueeze(3).to_broadcast([P, T, H, HD]), ALU.mult)
                e.wait_ge(g_pe.sem, n * 2 + 2)
                e.reg_add(general_n[e], general_n[e], 1)
                w = e.value_load(any_win[0:1, 1:2], min_val=0, max_val=NW - 1)
                row = acc[:, bass.ds(w, 1), :].rearrange("p a m -> p (a m)")
                op(e.tensor_tensor, row, row, any_sum, ALU.add)

            start = [windows_in, steps_in, win_out, zeros_out, acc_zero, *tables_out[l], *acc_cleared, *early_free,
                     *[lane.done_point() for lane in (pe, act, dve)]]
            for lane, body in ((sp, load_steps), (pool, gather_step), (pe, product_step), (act, exp_step), (dve, vector_step)):
                lane.wait(*start)
                if l == 0:
                    lane.queue.append(general_begin)
                if lane is sp:
                    lane.queue.append(load_steps)
                else:
                    lane.queue.append(lambda e, body=body: over_steps(e, body))
            acc_in["last"] = dve.do(nc.vector.memset, any_base[:], 0.0)

        general_n = {}

        def general_begin(e):
            general_n[e] = e.alloc_register("general_step")
            e.reg_mov(general_n[e], 0)

        begin([lane.general for lane in lanes])
        dve.queue.append(lambda e: e.memset(any_base[:], 0.0).then_inc(g_dve.sem, 1))
        for l in range(L):
            general_edges(l)
            pipeline([node_tile(l, j) for j in range(NT)], WORK - 1)
        outputs_written()

        begin([lane.regular for lane in lanes])
        for l in range(L):
            active, waiting = [], [node_tile(l, j) for j in range(NT)]

            def advance():
                active[:] = [g for g in active if next(g, True) is not True]

            for c in range(RING_KV):
                gather(l, c)
            for c in range(2):
                load_rel(c)
                load_queries(l, c)
            for c in range(2):
                onehotT(c)
                load_rel(c + 2)
            spread(0)
            load_queries(l, 2)
            onehot(0)
            for c in range(NC):
                if c + 1 < NC:
                    spread(c + 1)
                products(c)
                scores(c)
                weights_of(c)
                if c + 2 < NC:
                    onehotT(c + 2)
                if c + 3 < NC:
                    load_queries(l, c + 3)
                if c + 4 < NC:
                    load_rel(c + 4)
                if c + 1 < NC:
                    onehot(c + 1)
                advance()
                if c > 0:
                    accumulate(c - 1)
                messages(c)
                if c + RING_KV < NC:
                    gather(l, c + RING_KV)
                if c == NC - 1:
                    accumulate(c)
                elif c - LAG - CPT >= 0 and (c - LAG) % CPT == 0 and waiting and len(active) < WORK - 1:
                    active.append(waiting.pop(0))
                advance()
            while active or waiting:
                if waiting and len(active) < WORK - 1:
                    active.append(waiting.pop(0))
                advance()
            state.clear()
        outputs_written()

        with nc.Block() as block:
            block.sync(lambda e: sp.play(e, irregular[0:1, 0:1]))
            block.tensor(lambda e: pe.play(e, irregular[0:1, 0:1]))
            block.scalar(lambda e: act.play(e, irregular[0:1, 0:1]))
            block.vector(lambda e: dve.play(e, irregular[0:1, 0:1]))
            block.gpsimd(lambda e: pool.play(e, irregular[0:1, 0:1]))


_PARAMS = ["Wq", "bq", "Wk", "bk", "Wv", "bv", "Wo", "bo", "Wpos", "bpos", "Wdeg", "bdeg",
           "ln1_g", "ln1_b", "ln2_g", "ln2_b", "W1", "b1", "W2", "b2"]


def kernel(**inputs):
    import numpy as _np
    import concourse.bacc as _bacc
    from concourse.bass_utils import run_bass_kernel_spmd as _run

    nc = _bacc.Bacc("TRN2", target_bir_lowering=False, num_devices=1)
    arrays = {"x": _np.ascontiguousarray(inputs["x"])}
    arrays["src"] = _np.concatenate([_np.asarray(inputs["src"]), _np.full(EP - E, N, _np.int32)])
    arrays["dst"] = _np.concatenate([_np.asarray(inputs["dst"]), _np.full(EP - E, FAR, _np.int32)])
    for name in _PARAMS:
        arrays[name] = _np.ascontiguousarray(inputs["L0_gnn_" + name])
    args = [nc.dram_tensor(f"in_{k}", a.shape, mybir.dt.from_np(a.dtype), kind="ExternalInput").ap()
            for k, a in arrays.items()]
    args.append(nc.dram_tensor("out_0", (N, D), F32, kind="ExternalOutput").ap())
    graph_transformer(nc, *args)
    r = _run(nc, [{f"in_{k}": a for k, a in arrays.items()}], core_ids=[0])
    return r.results[0]["out_0"]
```

```python
from contextlib import ExitStack

import concourse.bass as bass
from concourse import mybir

ALU = mybir.AluOpType
ACT = mybir.ActivationFunctionType
AX_X = mybir.AxisListType.X
F32 = mybir.dt.float32
I32 = mybir.dt.int32
BF16 = mybir.dt.bfloat16
U8 = mybir.dt.uint8

P = 128
N, D, H, L, FF, E = 6250, 128, 8, 2, 512, 200000
HD = D // H
NT = -(-N // P)
NP = NT * P
LAST = N - (NT - 1) * P
T = 8
CH = T * P
NC = -(-E // CH)
EP = NC * CH
HALF = P // 2
NW = (N - 1) // HALF + 1
QROWS = (NW - 1) * HALF + P
MW = D + H
FC = FF // P
QKV = 3 * D
FAR = 1 << 14
OUTSIDE = 255
LIMIT = 50.0
EPS = 1e-5
RING_KV = 4
WORK = 5
LAG = 1
EARLY = 4
CPT = -(-P * E // (N * CH))
HG = 32
HEAD_START = 8
OUT_TILES = 6
NEWTON = 3
RSQRT_MAGIC = float(0x5F3759DF)


class Counter:

    def __init__(self, sem):
        self.sem, self.value = sem, 0


class Lane:

    def __init__(self, done):
        self.done, self.queue, self.seen = done, [], {}
        self.before, self.regular, self.general = self.queue, [], []

    def done_point(self):
        return self.done, self.done.value

    def wait(self, *points):
        for counter, value in points:
            if self.seen.get(counter, 0) < value:
                self.seen[counter] = value
                self.queue.append(lambda e, s=counter.sem, v=value: e.wait_ge(s, v))

    def do(self, instruction, *args, after=(), **kw):
        self.wait(*after)
        self.done.value += 1
        self.queue.append(lambda e: instruction(*args, **kw).then_inc(self.done.sem, 1))
        return self.done, self.done.value

    def part(self, last, instruction, *args, after=(), **kw):
        if last:
            return self.do(instruction, *args, after=after, **kw)
        self.wait(*after)
        self.queue.append(lambda e: instruction(*args, **kw))

    def dma(self, counter, start, *args, after=(), **kw):
        self.wait(*after)
        counter.value += 16
        self.queue.append(lambda e: start(*args, **kw).then_inc(counter.sem, 16))
        return counter, counter.value

    def play(self, engine, irregular):
        for step in self.before:
            step(engine)
        is_irregular = engine.value_load(irregular, min_val=0, max_val=2 * NC)
        with engine.If(is_irregular == 0):
            for step in self.regular:
                step(engine)
        with engine.Else():
            for step in self.general:
                step(engine)


class Ring:

    def __init__(self, buffers):
        self.buffers, self.free, self.turn = buffers, [()] * len(buffers), 0

    def take(self):
        i = self.turn % len(self.buffers)
        self.turn += 1
        free, self.free[i] = self.free[i], None
        assert free is not None, "the buffer is still held"
        return i, self.buffers[i], free


def graph_transformer(nc, x, src, dst, Wq, bq, Wk, bk, Wv, bv, Wo, bo, Wpos, bpos, Wdeg, bdeg,
                      ln1_g, ln1_b, ln2_g, ln2_b, W1, b1, W2, b2, out):
    with ExitStack() as ctx:
        def sb(name, shape, dt=F32):
            return ctx.enter_context(nc.sbuf_tensor(name, shape, dt))

        def counter(name):
            return Counter(ctx.enter_context(nc.semaphore(name)))

        kv_table = [nc.dram_tensor(f"kv_table{l}", [NP, 2 * D], F32).ap() for l in range(L)]
        q_table = [nc.dram_tensor(f"q_table{l}", [QROWS, D], F32).ap() for l in range(L)]
        rel_table = nc.dram_tensor("rel_table", [EP], U8).ap()
        win_table = nc.dram_tensor("win_table", [NW, 2], I32).ap()

        x_all = sb("x_all", [P, NT, D])
        acc = sb("acc", [P, NW, MW])
        kv_ring = sb("kv_ring", [P, RING_KV, T, 2 * D])
        scratch = sb("scratch", [P, 5 * CH + 2 * T * MW])
        src_idx = sb("src_idx", [P, NC * T], I32)
        rel = sb("rel", [P, NC, T], U8)
        rel_b = sb("rel_b", [P, 2, CH], U8)
        q_win = sb("q_win", [P, 2, D])
        att = sb("att", [P, 2, T, H])
        att_ok = sb("att_ok", [P, T, H])
        att_clip = sb("att_clip", [P, T, H])
        work = sb("work", [P, WORK, 5 * P + QKV + MW + 32])
        w_qkv = sb("w_qkv", [P, L, QKV])
        b_qkv = sb("b_qkv", [P, L, QKV])
        w_pos = sb("w_pos", [P, L, D])
        w_o = sb("w_o", [P, L, D])
        w_1 = sb("w_1", [P, L, FF])
        w_2 = sb("w_2", [P, L, FC, D])
        w_deg = sb("w_deg", [NT, D])
        wz = sb("wz", [P, QKV])
        cols = sb("cols", [P, L, 8 + FC])
        rows = sb("rows", [1, L, 2, D])
        zero_rows = sb("zero_rows", [QROWS - NP, D])
        ident = sb("ident", [P, P])
        down = sb("down", [P, P])
        up = sb("up", [P, P])
        ones = sb("ones", [P, P])
        irregular = sb("irregular", [1, 1], I32)
        passes = sb("passes", [1, NC], I32)
        steps = sb("steps", [1, 1], I32)
        any_idx = sb("any_idx", [P, T], I32)
        any_dst = sb("any_dst", [P, T], I32)
        any_rel = sb("any_rel", [P, T])
        any_win = sb("any_win", [P, 2], I32)
        any_base = sb("any_base", [P, 1])
        win_rows = sb("win_rows", [1, NW, 2], I32)
        iota_i = sb("iota_i", [P, P], I32)
        iota = sb("iota", [P, P])
        part = sb("part", [P, 1])
        neg_part = sb("neg_part", [P, 1])
        small = sb("small", [P, 2])
        window = sb("window", [1, NC], I32)
        deg_z = sb("deg_z", [P, NT])
        deg_zT = sb("deg_zT", [NT, P])
        n_bufs = 0

        def carve(size):
            nonlocal n_bufs
            n_bufs += size
            return scratch[:, n_bufs - size:n_bufs]

        onehot_ring = Ring([carve(CH).rearrange("p (t j) -> p t j", t=T) for _ in range(2)])
        onehotT_ring = Ring([carve(CH) for _ in range(2)])
        prod = carve(CH)
        msg_ring = Ring([carve(T * MW).rearrange("p (t m) -> p t m", t=T) for _ in range(2)])
        accf = acc[:].rearrange("p w m -> p (w m)")
        in_acc = NW * MW // QKV

        def qkv_early(lo, hi):
            mem, first = (accf, 0) if lo < in_acc else (scratch, in_acc)
            return mem[:, (lo - first) * QKV:(hi - first) * QKV].rearrange("p (j n) -> p j n", n=QKV)

        spare = scratch[:, (NT - in_acc) * QKV:]
        src_lo = spare[:, 0:NC * T // 2].bitcast(BF16)
        stat = spare[:, NC * T // 2:NC * T // 2 + 14 * NT]
        deg_w = stat[:, 0:6 * NT]
        hist = kv_ring[:].rearrange("p a b c -> p (a b c)").bitcast(BF16)
        n_lo, n_hi = HALF * HG, NP // HALF * HG
        lo_ring = Ring([hist[:, i * n_lo:(i + 1) * n_lo].rearrange("p (v g) -> p v g", g=HG) for i in range(2)])
        hi_ring = Ring([hist[:, 2 * n_lo + i * n_hi:2 * n_lo + (i + 1) * n_hi].rearrange("p (v g) -> p v g", g=HG)
                        for i in range(2)])
        iota_rep = hist[:, 2 * (n_lo + n_hi):2 * n_lo + 3 * n_hi].rearrange("p (v g) -> p v g", g=HG)
        src_hi = hist[:, 2 * n_lo + 3 * n_hi:2 * n_lo + 3 * n_hi + NC * T]
        src_digits = [hist[:, 2 * i * NC * T:2 * (i + 1) * NC * T].bitcast(I32) for i in range(2)]
        by_chunk = sb("by_chunk", [1, 8, NC])
        first_i, last_i, base_i = (by_chunk[:, i, :].bitcast(I32) for i in range(3))
        base = by_chunk[:, 3, :]
        one_row = by_chunk[:, 4:8, :]

        psum = ctx.enter_context(nc.psum_tensor("psum", [P, 8, 512], F32))
        q_edge_ring = Ring([psum[:, 2 * i:2 * i + 2, :].rearrange("p b n -> p (b n)") for i in range(2)])
        sum_ring = Ring([psum[:, 4, 0:MW]])
        node_ring = Ring([psum[:, 5 + i, :] for i in range(3)])
        early_ring = Ring([psum[:, i, :] for i in range(5)])

        sp, pe, act, dve, pool = (Lane(counter(n)) for n in ("sp_done", "pe_done", "act_done", "dve_done", "pool_done"))
        c_const = counter("weights_in")
        c_x = counter("x_in")
        c_src, c_src_any = counter("src_in"), counter("src_in_any_order")
        c_dst, c_bounds = counter("dst_in"), counter("bounds_in")
        c_rel_out = counter("rel_out")
        c_q_out, c_kv_out = ([counter(f"{n}_out{i}") for i in range(WORK)] for n in ("q", "kv"))
        c_tables = [counter(f"first_tables_out{i}") for i in range(4)]
        c_zero = counter("zero_rows_out")
        c_win = counter("win_table_out")
        g_in, g_rows = counter("general_in"), counter("general_gathered")
        g_dve, g_pe, g_act = (counter(f"general_{n}") for n in ("dve", "pe", "act"))
        c_kv = [counter(f"gathered{i}") for i in range(RING_KV)]
        c_rel = [counter(f"rel_in{i}") for i in range(2)]
        c_qwin = [counter(f"q_win_in{i}") for i in range(2)]
        c_self = [counter(f"self_in{i}") for i in range(WORK)]
        c_xin = [counter(f"x_again{i}") for i in range(WORK)]
        c_out = [counter(f"out{i}") for i in range(WORK)]

        x_full = x[0:(NT - 1) * P, :].rearrange("(j p) f -> p j f", p=P)
        pad_x = dve.do(nc.vector.memset, x_all[:, NT - 1, :], 0.0)
        src_any_in = sp.dma(c_src_any, nc.sync.dma_start, src_idx[:], src.rearrange("(p k) -> p k", p=P))
        sp.dma(c_x, nc.sync.dma_start, x_all[:, 0:NT - 1, :], x_full)
        x_in = sp.dma(c_x, nc.sync.dma_start, x_all[0:LAST, NT - 1, :], x[(NT - 1) * P:N, :], after=[pad_x])

        def const(to, what):
            sp.dma(c_const, nc.sync.dma_start, to, what, allow_slow_non_contiguous=True)

        for l in range(L):
            for i, (W, b) in enumerate(((Wq, bq), (Wk, bk), (Wv, bv))):
                const(w_qkv[:, l, i * D:(i + 1) * D], W[l])
                const(b_qkv[:, l, i * D:(i + 1) * D], b[l].partition_broadcast(P))
            const(w_pos[:, l, :], Wpos[l])
            const(w_o[:, l, :], Wo[l])
            const(w_1[:, l, :], W1[l])
            const(w_2[:, l, :, :], W2[l].rearrange("(c p) n -> p c n", p=P))
            for i, v in enumerate((bpos, bdeg, ln1_g, ln1_b, ln2_g, ln2_b)):
                const(cols[:, l, i:i + 1], v[l].rearrange("(p a) -> p a", a=1))
            const(cols[:, l, 7:8], Wdeg[l, 0].rearrange("(p a) -> p a", a=1))
            const(cols[:, l, 8:8 + FC], b1[l].rearrange("(c p) -> p c", p=P))
            const(rows[0:1, l, 0, :], bo[l:l + 1, :])
            const(rows[0:1, l, 1, :], b2[l:l + 1, :])
        const(w_deg[:], Wdeg[1, 0].partition_broadcast(NT))
        weights_in = c_const, c_const.value
        chunks = dst.rearrange("(a c n) -> a c n", a=1, n=CH)
        act.dma(c_bounds, nc.scalar.dma_start, first_i[0:1, :].unsqueeze(2), chunks[:, :, 0:1],
                                             allow_slow_non_contiguous=True)
        act.dma(c_bounds, nc.scalar.dma_start, last_i[0:1, 0:NC - 1].unsqueeze(2), chunks[:, 0:NC - 1, CH - 1:CH],
                                             allow_slow_non_contiguous=True)
        act.dma(c_bounds, nc.scalar.dma_start, last_i[0:1, NC - 1:NC], dst[E - 1:E].rearrange("(a b) -> a b", a=1))
        bounds_in = c_bounds, c_bounds.value

        a = pool.do(nc.gpsimd.iota, iota_i[:], pattern=[[1, P]], base=0, channel_multiplier=0)
        iota_in = dve.do(nc.vector.tensor_copy, iota[:], iota_i[:], after=[a])
        rep_in = dve.do(nc.vector.tensor_copy, iota_rep, iota_i[:, 0:NP // HALF].unsqueeze(2).to_broadcast([P, NP // HALF, HG]), after=[a])
        a = pool.do(nc.gpsimd.memset, ones[:], 1.0)
        for t_, off in ((ident, 0), (down, -HALF), (up, HALF)):
            shapes_in = pool.do(nc.gpsimd.affine_select, out=t_[:], in_=ones[:], pattern=[[1, P]], compare_op=ALU.is_equal, fill=0.0, base=-off,
                channel_multiplier=-1, after=[a])
        part_p = dve.do(nc.vector.tensor_tensor, wz[:, 0:P], iota[:], ident[:], ALU.mult, after=[iota_in, shapes_in])
        part_in = dve.do(nc.vector.tensor_reduce, part[:], wz[:, 0:P], AX_X, ALU.add, after=[part_p])
        neg_part_in = dve.do(nc.vector.tensor_scalar, neg_part[:], part[:], -1.0, None, ALU.mult, after=[part_in])
        pool.do(nc.gpsimd.memset, small[:, 0:1], EPS)
        small_in = pool.do(nc.gpsimd.memset, small[:, 1:2], 1.5)
        zero_in = pool.do(nc.gpsimd.memset, zero_rows[:], 0.0)
        for l in range(L):
            zeros_out = act.dma(c_zero, nc.scalar.dma_start, q_table[l][NP:QROWS, :], zero_rows[:], after=[zero_in])
        a = pool.do(nc.gpsimd.iota, win_rows[:, :, 0], pattern=[[HALF, NW]], base=0, channel_multiplier=0)
        b = pool.do(nc.gpsimd.iota, win_rows[:, :, 1], pattern=[[1, NW]], base=0, channel_multiplier=0)
        win_out = act.dma(c_win, nc.scalar.dma_start, win_table.rearrange("(a w) b -> a w b", a=1), win_rows[:], after=[a, b])
        def ws(slot):
            w = work[:, slot, :]
            f = {"row": w[:, 0:P], "col": w[:, P:2 * P], "g": w[:, 2 * P:2 * P + 4 * P], "qkv": w[:, 5 * P:5 * P + QKV]}
            o = 5 * P + QKV
            return f, w[:, o:o + MW], w[:, o + MW:o + MW + 32]

        a = dve.do(nc.vector.tensor_scalar, src_digits[0], src_idx[:], HALF - 1, None, ALU.bitwise_and, after=[src_any_in])
        b = dve.do(nc.vector.tensor_scalar, src_digits[1], src_idx[:], HALF.bit_length() - 1, None, ALU.logical_shift_right, after=[src_any_in])
        a = dve.do(nc.vector.tensor_copy, src_lo, src_digits[0], after=[a])
        digits_in = dve.do(nc.vector.tensor_copy, src_hi, src_digits[1], after=[b])
        dst_i = src_idx[:].rearrange("p (c t) -> p c t", t=T)
        dst_in = act.dma(c_dst, nc.scalar.dma_start, dst_i, dst.rearrange("(c p t) -> p c t", p=P, t=T), after=[digits_in])
        counts = psum[0:HALF, 6, 0:NP // HALF]
        n_steps = NC * T // HG

        def histogram():
            for s in range(n_steps):
                _, lo, lo_free = lo_ring.take()
                i, hi, hi_free = hi_ring.take()
                g = slice(s * HG, (s + 1) * HG)
                a = dve.do(nc.vector.tensor_tensor, lo, src_lo[:, g].unsqueeze(1).to_broadcast([P, HALF, HG]), iota_rep[:, 0:HALF, :], ALU.is_equal,
                    after=[digits_in, rep_in, *lo_free])
                a = dve.do(nc.vector.tensor_tensor, hi, src_hi[:, g].unsqueeze(1).to_broadcast([P, NP // HALF, HG]), iota_rep, ALU.is_equal,
                    after=[*hi_free])
                for k in range(HG):
                    b = pe.part(k == HG - 1, nc.tensor.matmul, counts, lo[:, :, k], hi[:, :, k],
                                start=s == 0 and k == 0, stop=s == n_steps - 1 and k == HG - 1, after=[a])
                lo_ring.free[i] = hi_ring.free[i] = [b]
                yield b

        h_steps = histogram()
        for _ in range(HEAD_START):
            next(h_steps)

        s1 = dve.do(nc.vector.tensor_scalar, w_qkv[:, :, 0:D], w_qkv[:, :, 0:D], HD ** -0.5, None, ALU.mult, after=[weights_in])
        s2 = dve.do(nc.vector.tensor_scalar, b_qkv[:, :, 0:D], b_qkv[:, :, 0:D], HD ** -0.5, None, ALU.mult, after=[weights_in])
        s3 = dve.do(nc.vector.tensor_tensor, w_pos[:], w_pos[:], ident[:].unsqueeze(1).to_broadcast([P, L, P]), ALU.add,
                    after=[weights_in, shapes_in])
        weights_in = dve.do(nc.vector.tensor_tensor, cols[:, :, 6:7], cols[:, :, 0:1], cols[:, :, 1:2], ALU.add, after=[weights_in, s1, s2, s3])

        a = dve.do(nc.vector.tensor_scalar, work[:, 0, 0:P], ones[:], cols[:, 0, 7:8], None, ALU.mult, after=[weights_in, shapes_in])
        wz_sum = pe.do(nc.tensor.matmul, psum[:, 7, 0:QKV], work[:, 0, 0:P], w_qkv[:, 0, :], start=True, stop=True, after=[a])

        def rsqrt(v, y, t, after):
            a = dve.do(nc.vector.tensor_scalar, t.bitcast(I32), v.bitcast(I32), 1, None, ALU.logical_shift_right, after=after)
            a = dve.do(nc.vector.tensor_scalar, y.bitcast(I32), t.bitcast(I32), -1.0, RSQRT_MAGIC, ALU.mult, ALU.add, after=[a])
            for _ in range(NEWTON):
                if v.shape[1] == 1:
                    a = dve.do(nc.vector.tensor_scalar, t, y, y, v, ALU.mult, ALU.mult, after=[a])
                else:
                    a = dve.do(nc.vector.tensor_tensor, t, y, y, ALU.mult, after=[a])
                    a = dve.do(nc.vector.tensor_tensor, t, t, v, ALU.mult, after=[a])
                a = dve.do(nc.vector.tensor_scalar, t, t, -0.5, 1.5, ALU.mult, ALU.add, after=[a])
                a = dve.do(nc.vector.tensor_tensor, y, y, t, ALU.mult, after=[a])
            return a

        raw = stat[:, 0:6 * NT].rearrange("p (j s) -> p j s", s=6)
        mv = stat[:, 6 * NT:8 * NT].rearrange("p (j s) -> p j s", s=2)
        var0, rstd0, tmp0, shift0 = (stat[:, (8 + i) * NT:(9 + i) * NT] for i in range(4))
        for j in range(NT):
            a = dve.do(nc.vector.bn_stats, raw[:, j, :], x_all[:, j, :], after=[x_in])
        for j in range(NT):
            b = dve.do(nc.vector.bn_aggr, mv[:, j, :], raw[:, j, :], after=[a])
        a = dve.do(nc.vector.tensor_scalar, var0, mv[:, :, 1], EPS, None, ALU.add, after=[b])
        a = rsqrt(var0, rstd0, tmp0, [a])
        b = dve.do(nc.vector.tensor_tensor, shift0, mv[:, :, 0], rstd0, ALU.mult, after=[a])
        stats0 = dve.do(nc.vector.tensor_scalar, shift0, shift0, -1.0, None, ALU.mult, after=[b])

        wz_in = dve.do(nc.vector.tensor_copy, wz[:], psum[:, 7, 0:QKV], after=[wz_sum])

        def chunk_windows():
            shift = HALF.bit_length() - 1
            a = dve.do(nc.vector.tensor_scalar, window[:], first_i, shift, None, ALU.logical_shift_right, after=[bounds_in])
            a = dve.do(nc.vector.tensor_scalar, base_i, window[:], shift, None, ALU.logical_shift_left, after=[a])
            a = dve.do(nc.vector.tensor_copy, base, base_i, after=[a])
            windows_in = a
            a = dve.do(nc.vector.tensor_tensor, passes[:], last_i, base_i, ALU.subtract, after=[a])
            a = dve.do(nc.vector.tensor_scalar, passes[:], passes[:], P.bit_length() - 1, None, ALU.logical_shift_right, after=[a])
            wide = one_row[:, 0, :]
            a = dve.do(nc.vector.tensor_copy, wide, passes[:], after=[a])
            b = dve.do(nc.vector.tensor_scalar, passes[:], wide, 1.0, None, ALU.add, after=[a])
            a = dve.do(nc.vector.tensor_scalar, one_row[:, 1, :], wide, 1.0, None, ALU.add, after=[a])
            c = dve.do(nc.vector.tensor_reduce, one_row[:, 2, 0:1], one_row[:, 1, :], AX_X, ALU.add, after=[a])
            steps_in = dve.do(nc.vector.tensor_copy, steps[:], one_row[:, 2, 0:1], after=[c])
            turns = range(CPT + LAG, NC, CPT)
            late_row = one_row[:, 3, 0:len(turns)]
            d = dve.do(nc.vector.tensor_scalar, late_row, iota[0:1, 0:len(turns)], float(P), float(P), ALU.mult, ALU.add, after=[iota_in])
            d = dve.do(nc.vector.tensor_tensor, late_row, first_i[:, CPT + LAG:NC:CPT], late_row, ALU.is_lt, after=[bounds_in, d])
            d = dve.do(nc.vector.tensor_reduce, one_row[:, 2, 1:2], late_row, AX_X, ALU.add, after=[d])
            d = dve.do(nc.vector.scalar_tensor_tensor, out=one_row[:, 2, 2:3], in0=one_row[:, 2, 0:1], scalar=-float(NC),
                       in1=one_row[:, 2, 1:2], op0=ALU.add, op1=ALU.add, after=[c, d])
            plan_in = dve.do(nc.vector.tensor_copy, irregular[:], one_row[:, 2, 2:3], after=[d])
            a = b
            i, ps, free = early_ring.take()
            a = pe.do(nc.tensor.matmul, ps[:, 0:NC], ones[0:1, :], base, start=True, stop=True, after=[a, shapes_in, *free])
            whole = src_idx[:].bitcast(F32)
            a = dve.do(nc.vector.tensor_tensor, whole.rearrange("p (c t) -> p c t", t=T), dst_i,
                       ps[:, 0:NC].unsqueeze(2).to_broadcast([P, NC, T]), ALU.subtract, after=[a, dst_in])
            early_ring.free[i] = [a]
            rel_in = dve.do(nc.vector.tensor_scalar, rel[:].rearrange("p c t -> p (c t)"), whole, float(OUTSIDE), None, ALU.min, after=[a])
            rel_out = act.dma(c_rel_out, nc.scalar.dma_start, rel_table.rearrange("(c p t) -> p c t", p=P, t=T), rel[:],
                allow_slow_non_contiguous=True, after=[rel_in])
            src_in = act.dma(c_src, nc.scalar.dma_start, src_idx[:].rearrange("p (c t) -> p c t", t=T),
                             src.rearrange("(c p t) -> p c t", p=P, t=T), after=[rel_in])
            return windows_in, steps_in, plan_in, rel_in, rel_out, src_in

        qkv_early_in = [None] * NT

        def transposed(xhat, ring, hT, after, g_col, b_col):
            i, ps, free = ring.take()
            a = pe.do(nc.tensor.transpose, ps[:, 0:P], xhat, ident[:], after=[*after, shapes_in, *free])
            yield
            a = act.do(nc.scalar.activation, hT, ps[:, 0:P], ACT.Identity, scale=g_col, bias=b_col, after=[a, weights_in])
            ring.free[i] = [a]
            yield a

        work_free = [[wz_in]] + [[] for _ in range(WORK - 1)]
        work_turn = [0]

        def take_work():
            s = work_turn[0] % WORK
            work_turn[0] += 1
            return s, work_free[s]

        def early(j):
            s, free = take_work()
            f, _, _ = ws(s)
            a = act.do(nc.scalar.activation, f["row"], x_all[:, j, :], ACT.Identity, scale=rstd0[:, j:j + 1], bias=shift0[:, j:j + 1],
                       after=[stats0, *free])
            yield
            for a in transposed(f["row"], early_ring, f["col"], [a], cols[:, 0, 2:3], cols[:, 0, 3:4]):
                yield
            i, ps, free = early_ring.take()
            a = pe.do(nc.tensor.matmul, ps[:, 0:P], w_pos[:, 0, :], f["col"], start=True, stop=True, after=[a, *free])
            yield
            a = act.do(nc.scalar.activation, f["row"], ps[:, 0:P], ACT.Identity, bias=cols[:, 0, 6:7], after=[a])
            early_ring.free[i] = [a]
            yield
            i, ps, free = early_ring.take()
            a = pe.do(nc.tensor.matmul, ps[:, 0:QKV], f["row"], w_qkv[:, 0, :], start=True, stop=True, after=[a, *free])
            yield
            row = qkv_early(j, j + 1)[:, 0, :]
            a = act.do(nc.scalar.copy, row, ps[:, 0:QKV], after=[a])
            early_ring.free[i] = [a]
            work_free[s] = [a]
            qkv_early_in[j] = pool.do(nc.gpsimd.tensor_tensor, row, row, b_qkv[:, 0, :], ALU.add, after=[a])

        def pipeline(generators, width, between=None):
            waiting, active = list(generators), []
            while waiting or active:
                if waiting and len(active) < width:
                    active.append(waiting.pop(0))
                active = [g for g in active if next(g, True) is not True]
                if between is not None:
                    next(between, None)

        chunk_points = []

        def beside():
            for n, _ in enumerate(h_steps):
                if n == n_steps // 3:
                    chunk_points.extend(chunk_windows())
                for _ in range(2 + n % 2):
                    yield

        pipeline([early(j) for j in range(NT)], WORK - 1, beside())
        windows_in, steps_in, plan_in, rel_in, rel_out, src_in = chunk_points
        for _ in h_steps:
            pass
        hist_done = (pe.done, pe.done.value)

        dw = [deg_w[:, i * NT:(i + 1) * NT] for i in range(5)]
        valid, deg, dev, sq, one = dw[0], dw[1], dw[2], dw[3], dw[4]
        a = pool.do(nc.gpsimd.affine_select, out=valid, in_=ones[:, 0:NT], pattern=[[-P, NT]], compare_op=ALU.is_ge,
                                              fill=0.0, base=N - 1, channel_multiplier=-1, after=[shapes_in, part_in])
        halves = stat[0:HALF, 12 * NT:14 * NT]
        b = dve.do(nc.vector.tensor_copy, halves, counts, after=[hist_done])
        halves = halves.rearrange("p (j h) -> p j h", h=2)
        pe.part(False, nc.tensor.matmul, psum[:, 7, 0:NT], ident[0:HALF, :], halves[:, :, 0], start=True, stop=False, after=[b])
        hist_done = pe.do(nc.tensor.matmul, psum[:, 7, 0:NT], up[0:HALF, :], halves[:, :, 1], start=False, stop=True)
        b = dve.do(nc.vector.scalar_tensor_tensor, out=deg, in0=psum[:, 7, 0:NT], scalar=1.0, in1=valid, op0=ALU.add, op1=ALU.mult, after=[a, hist_done, part_in])
        a = dve.do(nc.vector.tensor_reduce, one[:, 0:1], deg, AX_X, ALU.add, after=[b])
        total = psum[:, 7, 0:1]
        a = pe.do(nc.tensor.matmul, total, ones[:], one[:, 0:1], start=True, stop=True, after=[a])
        a = dve.do(nc.vector.tensor_scalar, one[:, 1:2], total, -1.0 / N, None, ALU.mult, after=[a])
        a = dve.do(nc.vector.scalar_tensor_tensor, out=dev, in0=deg, scalar=one[:, 1:2], in1=valid, op0=ALU.add, op1=ALU.mult, after=[a])
        a = dve.do(nc.vector.tensor_tensor, sq, dev, dev, ALU.mult, after=[a])
        a = dve.do(nc.vector.tensor_reduce, one[:, 2:3], sq, AX_X, ALU.add, after=[a])
        a = pe.do(nc.tensor.matmul, total, ones[:], one[:, 2:3], start=True, stop=True, after=[a])
        a = dve.do(nc.vector.tensor_scalar, one[:, 3:4], total, 1.0 / (N - 1), None, ALU.mult, after=[a])
        a = rsqrt(one[:, 3:4], one[:, 4:5], one[:, 5:6], [a])
        a = dve.do(nc.vector.tensor_scalar, one[:, 6:7], one[:, 4:5], one[:, 3:4], 1e-6, ALU.mult, ALU.add, after=[a])
        a = dve.do(nc.vector.reciprocal, one[:, 7:8], one[:, 6:7], after=[a])
        a = dve.do(nc.vector.tensor_scalar, deg_z[:], dev, one[:, 7:8], None, ALU.mult, after=[a])
        a = pe.do(nc.tensor.transpose, psum[0:NT, 7, 0:P], deg_z[:], ident[:], after=[a])
        deg_in = dve.do(nc.vector.tensor_copy, deg_zT[:], psum[0:NT, 7, 0:P], after=[a])
        node_ring.free = [[deg_in]] * 3

        def qkv_tile(l, j, s, xpT, after, ring):
            f, _, _ = ws(s)
            i, ps, free = ring.take()
            a = pe.do(nc.tensor.matmul, ps[:, 0:QKV], xpT, w_qkv[:, l, :], start=True, stop=True, after=[*after, *free])
            yield
            a = dve.do(nc.vector.tensor_tensor, f["qkv"], ps[:, 0:QKV], b_qkv[:, l, :], ALU.add, after=[a])
            ring.free[i] = [a]
            rows_ = slice(j * P, (j + 1) * P)
            kv = sp.dma(c_kv_out[s], nc.sync.dma_start, kv_table[l][rows_, :], f["qkv"][:, D:QKV], after=[a])
            q = sp.dma(c_q_out[s], nc.sync.dma_start, q_table[l][rows_, :], f["qkv"][:, 0:D])
            work_free[s] = [q, kv]
            kv_out[l].append(kv)
            q_out[l].append(q)

        q_out, kv_out = [[], []], [[], []]

        starts = [*range(0, in_acc, OUT_TILES), *range(in_acc, NT, OUT_TILES)]
        queues = (sp, nc.sync.dma_start), (act, nc.scalar.dma_start)
        for to, cols_, points, slots in ((kv_table[0], slice(D, QKV), kv_out[0], c_tables[0:2]), (q_table[0], slice(0, D), q_out[0], c_tables[2:4])):
            for n, (lo, hi) in enumerate(zip(starts, [*starts[1:], NT])):
                for j in range(lo, hi):
                    row = qkv_early(j, j + 1)[:, 0, cols_]
                    last = dve.do(nc.vector.scalar_tensor_tensor, out=row, in0=wz[:, cols_], scalar=deg_z[:, j:j + 1], in1=row,
                                  op0=ALU.mult, op1=ALU.add, after=[deg_in, wz_in, qkv_early_in[j]])
                lane, start = queues[n % 2]
                points.append(lane.dma(slots[n % 2], start, to[lo * P:hi * P, :].rearrange("(j p) n -> p j n", p=P),
                                       qkv_early(lo, hi)[:, :, cols_], after=[last]))
            points[:] = points[-2:]
        before_edges = [*q_out[0], *kv_out[0], last, rel_out, hist_done, plan_in, act.done_point()]
        acc_zero = dve.do(nc.vector.memset, accf, 0.0, after=before_edges)

        lanes = (sp, pe, act, dve, pool)
        for lane in lanes:
            lane.wait(plan_in, steps_in)
        early_free = [p for r in early_ring.free for p in r]
        scratch_free = before_edges
        counters = [v for v in (*[lane.done for lane in lanes], *c_q_out, *c_kv_out, *c_kv, *c_rel, *c_qwin, *c_self, *c_xin, *c_out)]
        snapshot = ([v.value for v in counters], [dict(lane.seen) for lane in lanes], [list(w) for w in work_free],
                    [list(f) for f in node_ring.free], work_turn[0])
        kv_free, rel_free, qwin_free, att_free = [], [], [], []
        prod_free, ok_free, acc_cleared = [], [], []
        acc_in, state = {}, {}

        def begin(queues):
            values, seen, free, node_free, turn = snapshot
            for v, value in zip(counters, values):
                v.value = value
            for lane, s_, queue in zip(lanes, seen, queues):
                lane.seen, lane.queue = dict(s_), queue
            for b in range(WORK):
                work_free[b] = list(free[b])
            work_turn[0] = turn
            node_ring.free = [list(f) for f in node_free]
            for r in (q_edge_ring, sum_ring, onehot_ring, onehotT_ring, msg_ring):
                r.free, r.turn = [early_free + scratch_free] * len(r.buffers), 0
            kv_free[:] = [[hist_done]] * RING_KV
            rel_free[:], qwin_free[:], att_free[:] = [[], []], [[], []], [[], []]
            prod_free[:], ok_free[:], acc_cleared[:] = scratch_free, [], []
            acc_in["last"] = acc_zero
            del q_out[1][:], kv_out[1][:]
            state.clear()

        def load_rel(c):
            b = c % 2
            r = sp.dma(c_rel[b], nc.sync.dma_start, rel_b[:, b, :], rel_table[c * CH:(c + 1) * CH].partition_broadcast(P),
                       after=[rel_out, *rel_free[b]])
            state[c] = {"rel": r}

        def load_queries(l, c):
            b = c % 2

            def q_load():
                w = nc.sync.value_load(window[0:1, c:c + 1], min_val=0, max_val=NW - 1)
                return nc.sync.dma_start(q_win[:, b, :], q_table[l][bass.ds(w * HALF, P), :])
            state[c]["q"] = sp.dma(c_qwin[b], q_load, after=[windows_in, zeros_out, *q_out[l], *qwin_free[b]])

        def gather(l, c):
            k = c % RING_KV
            pool.wait(src_in, *kv_out[l], *kv_free[k])
            for t in range(T):
                g = pool.dma(c_kv[k], nc.gpsimd.indirect_dma_start, kv_ring[:, k, t, :], None, kv_table[l],
                    bass.IndirectOffsetOnAxis(ap=src_idx[:, c * T + t:c * T + t + 1], axis=0))
            state.setdefault(("g", c), g)
            state[("g", c)] = g

        def exp_and_ln():
            act.queue.append(lambda e: e.preload_act_table_set("natural_log_exp_and_others"))

        def onehot(c):
            i, s_, free = onehot_ring.take()
            a = dve.do(nc.vector.tensor_tensor, s_, rel[:, c, :].unsqueeze(2).to_broadcast([P, T, P]), iota[:].unsqueeze(1).to_broadcast([P, T, P]),
                ALU.is_equal, after=[rel_in, iota_in, *free])
            state[c].update(S=s_, S_i=i, S_in=a)

        def onehotT(c):
            st = state[c]
            i, sT, free = onehotT_ring.take()
            a = act.do(nc.scalar.activation, sT, rel_b[:, c % 2, :], ACT.Abs, bias=neg_part[:], after=[st["rel"], neg_part_in, *free])
            rel_free[c % 2] = [a]
            a = act.do(nc.scalar.activation, sT, sT, ACT.Relu, bias=1.0, scale=-1.0, after=[a])
            st.update(ST=sT.rearrange("p (m t) -> p m t", t=T), ST_i=i, ST_in=a)

        def spread(c):
            st = state[c]
            i, ps, free = q_edge_ring.take()
            pe.wait(st["ST_in"], st["q"], *free)
            for t in range(T):
                a = pe.part(t == T - 1, nc.tensor.matmul, ps[:, t * P:(t + 1) * P], st["ST"][:, :, t], q_win[:, c % 2, :],
                            start=True, stop=True)
            onehotT_ring.free[st["ST_i"]] = [a]
            qwin_free[c % 2] = [a]
            st.update(qe=ps, qe_i=i, qe_in=a)

        def products(c):
            st = state[c]
            k = c % RING_KV
            a = dve.do(nc.vector.tensor_tensor, prod.rearrange("p (t d) -> p t d", t=T), st["qe"].rearrange("p (t d) -> p t d", t=T),
                                                 kv_ring[:, k, :, 0:D], ALU.mult,
                       after=[st["qe_in"], state[("g", c)], *prod_free])
            q_edge_ring.free[st["qe_i"]] = [a]
            st.update(prod_in=a)

        def scores(c):
            st = state[c]
            b = c % 2
            a = dve.do(nc.vector.tensor_reduce, att[:, b, :, :].rearrange("p t h -> p (t h)"),
                                                 prod.rearrange("p (g d) -> p g d", d=HD), AX_X, ALU.add,
                       after=[st["prod_in"], *att_free[b]])
            prod_free[:] = [a]
            d = dve.do(nc.vector.tensor_tensor, att_ok[:], att[:, b], att[:, b], ALU.is_equal, after=[a, *ok_free])
            a = dve.do(nc.vector.tensor_scalar, att_clip[:], att[:, b], -LIMIT, LIMIT, ALU.max, ALU.min, after=[a, *ok_free])
            a = dve.do(nc.vector.tensor_tensor, att[:, b], att_clip[:], att_ok[:], ALU.mult, after=[a, d])
            ok_free[:] = [a]
            st.update(att_in=a)

        def weights_of(c):
            st = state[c]
            b = c % 2
            mi, m_, free = msg_ring.take()
            a = act.do(nc.scalar.activation, m_[:, :, D:MW], att[:, b], ACT.Exp, after=[st["att_in"], *free])
            att_free[b] = [a]
            st.update(m=m_, m_i=mi, ex_in=a)

        def messages(c):
            st = state[c]
            m_ = st["m"]
            k = c % RING_KV
            a = dve.do(nc.vector.tensor_tensor, m_[:, :, 0:D].rearrange("p t (h d) -> p t h d", d=HD),
                kv_ring[:, k, :, D:2 * D].rearrange("p t (h d) -> p t h d", d=HD),
                m_[:, :, D:MW].unsqueeze(3).to_broadcast([P, T, H, HD]), ALU.mult, after=[st["ex_in"]])
            kv_free[k] = [a]
            i, ps, free = sum_ring.take()
            pe.wait(a, st["S_in"], *free)
            for t in range(T):
                b = pe.part(t == T - 1, nc.tensor.matmul, ps, st["S"][:, t, :], m_[:, t, :], start=t == 0, stop=t == T - 1)
            onehot_ring.free[st["S_i"]] = [b]
            msg_ring.free[st["m_i"]] = [b]
            st.update(sum=ps, sum_i=i, sum_in=b)

        def accumulate(c):
            st = state.pop(c)

            def add():
                w = nc.vector.value_load(window[0:1, c:c + 1], min_val=0, max_val=NW - 1)
                row = acc[:, bass.ds(w, 1), :].rearrange("p a m -> p (a m)")
                return nc.vector.tensor_tensor(row, row, st["sum"], ALU.add)
            a = dve.do(add, after=[st["sum_in"], acc_in["last"], *acc_cleared])
            acc_in["last"] = a
            acc_in["chunks"] = c + 1
            sum_ring.free[st["sum_i"]] = [a]

        def statistics(j, tiny, after):
            a = dve.do(nc.vector.bn_stats, tiny[:, 0:6], x_all[:, j, :], after=after)
            return dve.do(nc.vector.bn_aggr, tiny[:, 6:8], tiny[:, 0:6], after=[a])

        def normalised(j, tiny, to, a):
            mean, v, y, t = (tiny[:, i:i + 1] for i in (6, 8, 9, 10))
            a = act.do(nc.scalar.activation, v, tiny[:, 7:8], ACT.Identity, bias=small[:, 0:1], after=[a, small_in])
            a = act.do(nc.scalar.activation, t, v, ACT.Ln, after=[a])
            a = act.do(nc.scalar.activation, y, t, ACT.Exp, scale=-0.5, after=[a])
            a = act.do(nc.scalar.activation, t, y, ACT.Square, after=[a])
            a = act.do(nc.scalar.activation, t, t, ACT.Copy, scale=v, after=[a])
            a = act.do(nc.scalar.activation, t, t, ACT.Identity, scale=-0.5, bias=small[:, 1:2], after=[a])
            a = act.do(nc.scalar.activation, y, y, ACT.Copy, scale=t, after=[a])
            yield
            a = dve.do(nc.vector.tensor_scalar, to, x_all[:, j, :], mean, y, ALU.subtract, ALU.mult, after=[a])
            yield a

        def node_tile(l, j):
            s, free = take_work()
            f, own, tiny = ws(s)
            rows_ = slice(j * P, (j + 1) * P)
            n_real = P if j < NT - 1 else LAST
            sp.dma(c_self[s], nc.sync.dma_start, f["qkv"][:, 0:D], q_table[l][rows_, :], after=[*q_out[l], *kv_out[l], *free])
            a = sp.dma(c_self[s], nc.sync.dma_start, f["qkv"][:, D:QKV], kv_table[l][rows_, :])
            yield
            yield
            sa, sok = tiny[:, 16:16 + H], tiny[:, 24:24 + H]
            a = dve.do(nc.vector.tensor_tensor, f["row"], f["qkv"][:, 0:D], f["qkv"][:, D:2 * D], ALU.mult, after=[a])
            a = dve.do(nc.vector.tensor_reduce, sa, f["row"].rearrange("p (h d) -> p h d", d=HD), AX_X, ALU.add, after=[a])
            b = dve.do(nc.vector.tensor_tensor, sok, sa, sa, ALU.is_equal, after=[a])
            a = dve.do(nc.vector.tensor_scalar, sa, sa, -LIMIT, LIMIT, ALU.max, ALU.min, after=[a, b])
            a = dve.do(nc.vector.tensor_tensor, sa, sa, sok, ALU.mult, after=[a, b])
            a = act.do(nc.scalar.activation, own[:, D:MW], sa, ACT.Exp, after=[a])
            yield
            a = dve.do(nc.vector.tensor_tensor, own[:, 0:D].rearrange("p (h d) -> p h d", d=HD),
                                                 f["qkv"][:, 2 * D:QKV].rearrange("p (h d) -> p h d", d=HD),
                                                 own[:, D:MW].unsqueeze(2).to_broadcast([P, H, HD]), ALU.mult, after=[a])
            x_in_again = None
            if l == L - 1:
                x_in_again = sp.dma(c_xin[s], nc.sync.dma_start, f["qkv"][0:n_real, D:2 * D], x[j * P:j * P + n_real, :], after=[a])
            yield
            while acc_in["chunks"] < min(CPT * (j + 1) + LAG, NC):
                yield
            i, ps, free = node_ring.take()
            parts = [(ident, acc[:, 2 * j, :])]
            if j > 0:
                parts.append((down, acc[:, 2 * j - 1, :]))
            if 2 * j + 1 < NW:
                parts.append((up, acc[:, 2 * j + 1, :]))
            pe.wait(a, acc_in["last"], *free)
            pe.part(False, nc.tensor.matmul, ps[:, 0:MW], ident[:], own, start=True, stop=False)
            for n, (m_, what) in enumerate(parts):
                a = pe.part(n == len(parts) - 1, nc.tensor.matmul, ps[:, 0:MW], m_[:], what, start=False,
                            stop=n == len(parts) - 1)
            yield
            if l + 1 < L:
                done = slice(max(2 * j - 1, 0), 2 * j + 1 if j < NT - 1 else NW)
                b = act.do(nc.scalar.memzero, acc[:, done, :], after=[a])
                acc_cleared[:] = [b]
            den = tiny[:, 0:H]
            b = dve.do(nc.vector.tensor_scalar, den, ps[:, D:MW], 1e-16, None, ALU.mult, after=[a])
            b = dve.do(nc.vector.tensor_tensor, den, den, ps[:, D:MW], ALU.add, after=[b])
            b = dve.do(nc.vector.reciprocal, den, den, after=[b])
            a = dve.do(nc.vector.tensor_tensor, f["row"].rearrange("p (h d) -> p h d", d=HD),
                                                 ps[:, 0:D].rearrange("p (h d) -> p h d", d=HD),
                                                 den.unsqueeze(2).to_broadcast([P, H, HD]), ALU.mult, after=[b])
            node_ring.free[i] = [a]
            yield
            i, ps, free = node_ring.take()
            a = pe.do(nc.tensor.transpose, ps[:, 0:P], f["row"], ident[:], after=[a, *free])
            yield
            a = act.do(nc.scalar.copy, f["col"], ps[:, 0:P], after=[a])
            node_ring.free[i] = [a]
            yield
            i, ps, free = node_ring.take()
            pe.part(False, nc.tensor.matmul, ps[:, 0:D], ones[0:1, :], rows[0:1, l, 0, :], start=True, stop=False, after=[a, *free])
            a = pe.do(nc.tensor.matmul, ps[:, 0:D], f["col"], w_o[:, l, :], start=False, stop=True)
            yield
            a = dve.do(nc.vector.tensor_tensor, x_all[:, j, :], x_all[:, j, :], ps[:, 0:D], ALU.add, after=[a])
            node_ring.free[i] = [a]
            b = statistics(j, tiny, [a])
            for a in normalised(j, tiny, f["row"], b):
                yield
            for a in transposed(f["row"], node_ring, f["col"], [a], cols[:, l, 4:5], cols[:, l, 5:6]):
                yield
            i, ps, free = node_ring.take()
            pe.wait(a, *free)
            for n in range(FC):
                a = pe.part(n == FC - 1, nc.tensor.matmul, ps[:, n * P:(n + 1) * P], w_1[:, l, n * P:(n + 1) * P], f["col"],
                            start=True, stop=True)
            yield
            for n in range(FC):
                g = act.do(nc.scalar.activation, f["g"][:, n * P:(n + 1) * P], ps[:, n * P:(n + 1) * P], ACT.Gelu,
                                                       bias=cols[:, l, 8 + n:9 + n], after=[a])
            node_ring.free[i] = [g]
            exp_and_ln()
            yield
            i, ps, free = node_ring.take()
            pe.part(False, nc.tensor.matmul, ps[:, 0:D], ones[0:1, :], rows[0:1, l, 1, :], start=True, stop=False, after=[g, *free])
            for n in range(FC):
                a = pe.part(n == FC - 1, nc.tensor.matmul, ps[:, 0:D], f["g"][:, n * P:(n + 1) * P], w_2[:, l, n, :],
                            start=False, stop=n == FC - 1)
            yield
            a = dve.do(nc.vector.tensor_tensor, x_all[:, j, :], x_all[:, j, :], ps[:, 0:D], ALU.add, after=[a])
            node_ring.free[i] = [a]
            if l + 1 < L:
                b = statistics(j, tiny, [a])
                for a in normalised(j, tiny, f["row"], b):
                    yield
                for a in transposed(f["row"], node_ring, f["col"], [a], cols[:, l + 1, 2:3], cols[:, l + 1, 3:4]):
                    yield
                b = act.do(nc.scalar.activation, f["g"][0:NT, 0:D], w_deg[:], ACT.Copy, scale=ident[0:NT, j:j + 1], after=[a])
                yield
                i, ps, free = node_ring.take()
                pe.part(False, nc.tensor.matmul, ps[:, 0:P], w_pos[:, l + 1, :], f["col"], start=True, stop=False, after=[a, *free])
                a = pe.do(nc.tensor.matmul, ps[:, 0:P], f["g"][0:NT, 0:D], deg_zT[:], start=False, stop=True, after=[b])
                yield
                a = act.do(nc.scalar.activation, f["row"], ps[:, 0:P], ACT.Identity, bias=cols[:, l + 1, 6:7], after=[a])
                node_ring.free[i] = [a]
                yield
                yield from qkv_tile(l + 1, j, s, f["row"], [a], node_ring)
            else:
                n = n_real
                a = dve.do(nc.vector.tensor_tensor, x_all[0:n, j, :], x_all[0:n, j, :], f["qkv"][0:n, D:2 * D], ALU.add, after=[a, x_in_again])
                b = statistics(j, tiny, [a])
                for a in normalised(j, tiny, f["col"], b):
                    yield
                a = sp.dma(c_out[s], nc.sync.dma_start, out[j * P:j * P + n, :], f["col"][0:n, :], after=[a])
                work_free[s] = [a]

        def outputs_written():
            sp.wait(*[(c, c.value) for c in (*c_out, *c_q_out, *c_kv_out)], rel_out, zeros_out, win_out)

        DVE_OPS = 11

        def general_edges(l):
            any_S, any_ST, any_dst_b = onehot_ring.buffers[0], onehotT_ring.buffers[0], onehot_ring.buffers[1]
            any_dst_b = any_dst_b.rearrange("p t j -> p (t j)").bitcast(I32)
            any_msg, any_q, any_sum = msg_ring.buffers[0], q_edge_ring.buffers[0], sum_ring.buffers[0]
            rows_in = kv_ring[:, 0, :, :]
            q0, score = q_win[:, 0, :], att[:, 0]
            N_IN = 5

            def load_steps(e):
                n = general_n[e]
                window_number = e.alloc_register(f"window_number{l}")
                with e.Fori(0, NC) as c:
                    chunk = e.snap(c)
                    w0 = e.value_load(window[0:1, bass.ds(chunk, 1)], min_val=0, max_val=NW - 1)
                    count = e.value_load(passes[0:1, bass.ds(chunk, 1)], min_val=1, max_val=NT)
                    e.reg_mov(window_number, w0)
                    with e.Fori(0, count):
                        e.wait_ge(g_dve.sem, e.snap(n) * DVE_OPS + 1)
                        w = e.snap(window_number, min_val=0, max_val=NW - 1)
                        edges = bass.ds(chunk * CH, CH)
                        for to, what in ((any_idx[:], src[edges].rearrange("(p t) -> p t", p=P)),
                                         (any_dst[:], dst[edges].rearrange("(p t) -> p t", p=P)),
                                         (any_dst_b, dst[edges].partition_broadcast(P)),
                                         (any_win[:], win_table[bass.ds(w, 1), :].rearrange("a b -> (a b)").partition_broadcast(P)),
                                         (q0, q_table[l][bass.ds(w * HALF, P), :])):
                            e.dma_start(to, what).then_inc(g_in.sem, 16)
                        e.reg_add(window_number, window_number, 2)
                        e.reg_add(n, n, 1)

            def over_steps(e, body):
                n = general_n[e]
                total = e.value_load(steps[0:1, 0:1], min_val=NC, max_val=NC + NW)
                with e.Fori(0, total):
                    body(e, e.snap(n))

            def gather_step(e, n):
                e.wait_ge(g_in.sem, n * (16 * N_IN) + 16 * N_IN)
                e.reg_add(general_n[e], general_n[e], 1)
                for t in range(T):
                    e.indirect_dma_start(rows_in[:, t, :], None, kv_table[l],
                                         bass.IndirectOffsetOnAxis(ap=any_idx[:, t:t + 1], axis=0)).then_inc(g_rows.sem, 16)

            def product_step(e, n):
                e.wait_ge(g_dve.sem, n * DVE_OPS + 5)
                e.wait_ge(g_in.sem, n * (16 * N_IN) + 16 * N_IN)
                ST = any_ST.rearrange("p (m t) -> p m t", t=T)
                for t in range(T):
                    last = e.matmul(any_q[:, t * P:(t + 1) * P], ST[:, :, t], q0, start=True, stop=True)
                last.then_inc(g_pe.sem, 1)
                e.wait_ge(g_dve.sem, n * DVE_OPS + 11)
                for t in range(T):
                    last = e.matmul(any_sum, any_S[:, t, :], any_msg[:, t, :], start=t == 0, stop=t == T - 1)
                last.then_inc(g_pe.sem, 1)
                e.reg_add(general_n[e], general_n[e], 1)

            def exp_step(e, n):
                e.wait_ge(g_dve.sem, n * DVE_OPS + 10)
                e.activation(any_msg[:, :, D:MW], score, ACT.Exp).then_inc(g_act.sem, 1)
                e.reg_add(general_n[e], general_n[e], 1)

            def vector_step(e, n):
                done = [1]

                def op(instruction, *args):
                    instruction(*args).then_inc(g_dve.sem, 1)
                    done[0] += 1
                    e.wait_ge(g_dve.sem, n * DVE_OPS + done[0])

                e.wait_ge(g_in.sem, n * (16 * N_IN) + 16 * N_IN)
                op(e.tensor_copy, any_base[:], any_win[:, 0:1])
                op(e.tensor_scalar, any_rel[:], any_dst[:], any_base[:], None, ALU.subtract)
                op(e.tensor_tensor, any_S, any_rel[:].unsqueeze(2).to_broadcast([P, T, P]),
                   iota[:].unsqueeze(1).to_broadcast([P, T, P]), ALU.is_equal)
                op(e.tensor_scalar, any_ST, any_dst_b, any_base[:], part[:], ALU.subtract, ALU.is_equal)
                e.wait_ge(g_pe.sem, n * 2 + 1)
                e.wait_ge(g_rows.sem, n * (16 * T) + 16 * T)
                op(e.tensor_tensor, prod.rearrange("p (t d) -> p t d", t=T), any_q.rearrange("p (t d) -> p t d", t=T),
                   rows_in[:, :, 0:D], ALU.mult)
                op(e.tensor_reduce, score.rearrange("p t h -> p (t h)"), prod.rearrange("p (g d) -> p g d", d=HD), AX_X, ALU.add)
                op(e.tensor_tensor, att_ok[:], score, score, ALU.is_equal)
                op(e.tensor_scalar, score, score, -LIMIT, LIMIT, ALU.max, ALU.min)
                op(e.tensor_tensor, score, score, att_ok[:], ALU.mult)
                e.wait_ge(g_act.sem, n + 1)
                op(e.tensor_tensor, any_msg[:, :, 0:D].rearrange("p t (h d) -> p t h d", d=HD),
                   rows_in[:, :, D:2 * D].rearrange("p t (h d) -> p t h d", d=HD),
                   any_msg[:, :, D:MW].unsqueeze(3).to_broadcast([P, T, H, HD]), ALU.mult)
                e.wait_ge(g_pe.sem, n * 2 + 2)
                e.reg_add(general_n[e], general_n[e], 1)
                w = e.value_load(any_win[0:1, 1:2], min_val=0, max_val=NW - 1)
                row = acc[:, bass.ds(w, 1), :].rearrange("p a m -> p (a m)")
                op(e.tensor_tensor, row, row, any_sum, ALU.add)

            start = [windows_in, steps_in, win_out, zeros_out, acc_zero, *q_out[l], *kv_out[l], *acc_cleared, *early_free,
                     *[lane.done_point() for lane in (pe, act, dve)]]
            for lane, body in ((sp, load_steps), (pool, gather_step), (pe, product_step), (act, exp_step), (dve, vector_step)):
                lane.wait(*start)
                if l == 0:
                    lane.queue.append(general_begin)
                if lane is sp:
                    lane.queue.append(load_steps)
                else:
                    lane.queue.append(lambda e, body=body: over_steps(e, body))
            acc_in["last"] = dve.do(nc.vector.memset, any_base[:], 0.0)
            acc_in["chunks"] = NC

        general_n = {}

        def general_begin(e):
            general_n[e] = e.alloc_register("general_step")
            e.reg_mov(general_n[e], 0)

        begin([lane.general for lane in lanes])
        dve.queue.append(lambda e: e.memset(any_base[:], 0.0).then_inc(g_dve.sem, 1))
        for l in range(L):
            exp_and_ln()
            general_edges(l)
            pipeline([node_tile(l, j) for j in range(NT)], WORK - 1)
        outputs_written()

        begin([lane.regular for lane in lanes])
        for l in range(L):
            active, waiting = [], [node_tile(l, j) for j in range(NT)]
            acc_in["chunks"] = 0

            def advance():
                active[:] = [g for g in active if next(g, True) is not True]

            exp_and_ln()
            for c in range(RING_KV):
                gather(l, c)
            for c in range(2):
                load_rel(c)
                load_queries(l, c)
            for c in range(2):
                onehotT(c)
                load_rel(c + 2)
            spread(0)
            load_queries(l, 2)
            onehot(0)
            for c in range(NC):
                if c + 1 < NC:
                    spread(c + 1)
                products(c)
                scores(c)
                weights_of(c)
                if c + 2 < NC:
                    onehotT(c + 2)
                if c + 3 < NC:
                    load_queries(l, c + 3)
                if c + 4 < NC:
                    load_rel(c + 4)
                if c + 1 < NC:
                    onehot(c + 1)
                advance()
                if c > 0:
                    accumulate(c - 1)
                messages(c)
                if c + RING_KV < NC:
                    gather(l, c + RING_KV)
                if c == NC - 1:
                    accumulate(c)
                elif waiting and len(active) < WORK - 1 and c + EARLY >= CPT * (NT - len(waiting) + 1) + LAG:
                    active.append(waiting.pop(0))
                advance()
            while active or waiting:
                if waiting and len(active) < WORK - 1:
                    active.append(waiting.pop(0))
                advance()
            state.clear()
        outputs_written()

        with nc.Block() as block:
            block.sync(lambda e: sp.play(e, irregular[0:1, 0:1]))
            block.tensor(lambda e: pe.play(e, irregular[0:1, 0:1]))
            block.scalar(lambda e: act.play(e, irregular[0:1, 0:1]))
            block.vector(lambda e: dve.play(e, irregular[0:1, 0:1]))
            block.gpsimd(lambda e: pool.play(e, irregular[0:1, 0:1]))


_PARAMS = ["Wq", "bq", "Wk", "bk", "Wv", "bv", "Wo", "bo", "Wpos", "bpos", "Wdeg", "bdeg",
           "ln1_g", "ln1_b", "ln2_g", "ln2_b", "W1", "b1", "W2", "b2"]


def kernel(**inputs):
    import numpy as _np
    import concourse.bacc as _bacc
    from concourse.bass_utils import run_bass_kernel_spmd as _run

    nc = _bacc.Bacc("TRN2", target_bir_lowering=False, num_devices=1)
    arrays = {"x": _np.ascontiguousarray(inputs["x"])}
    arrays["src"] = _np.concatenate([_np.asarray(inputs["src"]), _np.full(EP - E, N, _np.int32)])
    arrays["dst"] = _np.concatenate([_np.asarray(inputs["dst"]), _np.full(EP - E, FAR, _np.int32)])
    for name in _PARAMS:
        arrays[name] = _np.ascontiguousarray(inputs["L0_gnn_" + name])
    args = [nc.dram_tensor(f"in_{k}", a.shape, mybir.dt.from_np(a.dtype), kind="ExternalInput").ap()
            for k, a in arrays.items()]
    args.append(nc.dram_tensor("out_0", (N, D), F32, kind="ExternalOutput").ap())
    graph_transformer(nc, *args)
    r = _run(nc, [{f"in_{k}": a for k, a in arrays.items()}], core_ids=[0])
    return r.results[0]["out_0"]
```
